# Optimizing a Trainium2 kernel written in Bass

```python
import numpy as np
import jax
import jax.numpy as jnp

def _softmax(x, axis=-1):
    return jax.nn.softmax(x, axis=axis)

def _gelu(x):
    return jax.nn.gelu(x, approximate=True)

def _silu(x):
    return jax.nn.silu(x)

def _sigmoid(x):
    return jax.nn.sigmoid(x)

def _layernorm(x, axis=-1, eps=1e-05):
    m = jnp.mean(x, axis=axis, keepdims=True)
    v = jnp.var(x, axis=axis, keepdims=True)
    return (x - m) / jnp.sqrt(v + eps)

def _scatter_add(tgt, idx, src, axis=0):
    return tgt.at[idx].add(src)

def _segment_sum(src, seg, n):
    return jax.ops.segment_sum(src, seg, n)
kernel_name = 'mk_conv_preact_d2_conv_nchw384_r2_940166'

def setup_inputs(seed: int=0):
    np.random.seed(seed)
    _w = jnp.asarray

    def _rec_inputs():
        import jax
        import jax.numpy as jnp
        _gk = jax.random.key(seed)
        x = -0.0001476 + 0.9999 * jax.random.normal(jax.random.fold_in(_gk, 1), (32, 192, 56, 56), jnp.float32)
        return x
    x = _rec_inputs()

    def _L0_conv_setup():
        import jax, jax.numpy as jnp
        import numpy as np
        DIM = 192
        KERNEL = 31
        PAD = KERNEL // 2
        key = jax.random.key(seed)
        k1, k2 = jax.random.split(key)
        x = jax.random.normal(k1, (32, DIM, 56, 56), dtype=jnp.float32)
        weight = jax.random.normal(k2, (DIM, 1, KERNEL, KERNEL), dtype=jnp.float32)
        bias_term = jnp.zeros((DIM,), dtype=jnp.float32)
        return {'x': x, 'weight': weight, 'bias_term': bias_term}
    _L0_conv_all = _L0_conv_setup()
    _L0_conv_in = {k: v for k, v in _L0_conv_all.items() if k in ('weight', 'bias_term')}
    del _L0_conv_all

    def _L1_conv_setup():
        import jax, jax.numpy as jnp
        import numpy as np
        from jax import lax
        PLANES = 192
        N_POINTS = 4
        KERNEL_SIZE = 11
        INIT_RADIUS = 2.0 * (2.0 / KERNEL_SIZE)

        def _make_kernels(weight_coord, radius, weights):
            K = KERNEL_SIZE
            lin = jnp.linspace(-1.0, 1.0, K)
            gy, gx = jnp.meshgrid(lin, lin, indexing='ij')
            kernel_coord = jnp.stack([gy, gx], axis=0).reshape(2, K * K)
            diff = weight_coord[:, :, None, :] - kernel_coord.T[None, None, :, :]
            diff = jnp.transpose(diff, (0, 1, 3, 2)).reshape(1, N_POINTS, 2, K, K)
            d = jax.nn.relu(1.0 - jnp.abs(diff).sum(axis=2) / radius)
            kernels = jnp.matmul(weights, d.reshape(1, N_POINTS, K * K)).reshape(PLANES, K, K)
            kernels = jnp.flip(jnp.transpose(kernels, (0, 2, 1)), axis=1)
            return kernels
        key = jax.random.key(seed)
        k1, k2, k3 = jax.random.split(key, 3)
        x = jax.random.normal(k1, (16, PLANES, 32, 32), dtype=jnp.float32)
        weight_coord = jnp.clip(0.2 * jax.random.normal(k2, (1, N_POINTS, 2), dtype=jnp.float32), -1.0, 1.0)
        radius = jnp.full((1, N_POINTS, 1, 1), INIT_RADIUS, dtype=jnp.float32)
        weights = 0.02 * jax.random.normal(k3, (1, PLANES, N_POINTS), dtype=jnp.float32)
        return {'x': x, 'weight_coord': weight_coord, 'radius': radius, 'weights': weights}
    _L1_conv_all = _L1_conv_setup()
    _L1_conv_in = {k: v for k, v in _L1_conv_all.items() if k in ('weight_coord', 'radius', 'weights')}
    del _L1_conv_all
    return {'x': x, 'L0_conv_weight': _L0_conv_in['weight'], 'L0_conv_bias_term': _L0_conv_in['bias_term'], 'L1_conv_weight_coord': _L1_conv_in['weight_coord'], 'L1_conv_radius': _L1_conv_in['radius'], 'L1_conv_weights': _L1_conv_in['weights']}

def reference(x, L0_conv_weight, L0_conv_bias_term, L1_conv_weight_coord, L1_conv_radius, L1_conv_weights):
    import jax
    import jax.numpy as jnp

    def _L0_conv_ref(x, weight, bias_term):
        import jax, jax.numpy as jnp
        import numpy as np
        DIM = 192
        KERNEL = 31
        PAD = KERNEL // 2
        out = jax.lax.conv_general_dilated(x, weight, window_strides=(1, 1), padding=[(PAD, PAD), (PAD, PAD)], dimension_numbers=('NCHW', 'OIHW', 'NCHW'), feature_group_count=DIM)
        return out + bias_term[None, :, None, None]

    def _L1_conv_ref(x, weight_coord, radius, weights):
        import jax, jax.numpy as jnp
        import numpy as np
        from jax import lax
        PLANES = 192
        N_POINTS = 4
        KERNEL_SIZE = 11
        INIT_RADIUS = 2.0 * (2.0 / KERNEL_SIZE)

        def _make_kernels(weight_coord, radius, weights):
            K = KERNEL_SIZE
            lin = jnp.linspace(-1.0, 1.0, K)
            gy, gx = jnp.meshgrid(lin, lin, indexing='ij')
            kernel_coord = jnp.stack([gy, gx], axis=0).reshape(2, K * K)
            diff = weight_coord[:, :, None, :] - kernel_coord.T[None, None, :, :]
            diff = jnp.transpose(diff, (0, 1, 3, 2)).reshape(1, N_POINTS, 2, K, K)
            d = jax.nn.relu(1.0 - jnp.abs(diff).sum(axis=2) / radius)
            kernels = jnp.matmul(weights, d.reshape(1, N_POINTS, K * K)).reshape(PLANES, K, K)
            kernels = jnp.flip(jnp.transpose(kernels, (0, 2, 1)), axis=1)
            return kernels
        kernels = _make_kernels(weight_coord, radius, weights)
        pad = KERNEL_SIZE // 2
        out = lax.conv_general_dilated(x, kernels[:, None, :, :], window_strides=(1, 1), padding=[(pad, pad), (pad, pad)], dimension_numbers=('NCHW', 'OIHW', 'NCHW'), feature_group_count=PLANES)
        return out

    def _gn(v, G=32, eps=1e-05):
        B_, C_, H_, W_ = v.shape
        g = v.reshape(B_, G, C_ // G, H_, W_)
        m = jnp.mean(g, axis=(2, 3, 4), keepdims=True)
        s = jnp.var(g, axis=(2, 3, 4), keepdims=True)
        return ((g - m) / jnp.sqrt(s + eps)).reshape(v.shape)

    def _ln_c(v, eps=1e-06):
        m = jnp.mean(v, axis=1, keepdims=True)
        s = jnp.var(v, axis=1, keepdims=True)
        return (v - m) / jnp.sqrt(s + eps)

    def _ln_t(v, eps=1e-05):
        m = jnp.mean(v, axis=-1, keepdims=True)
        s = jnp.var(v, axis=-1, keepdims=True)
        return (v - m) / jnp.sqrt(s + eps)

    def _to_tokens(v):
        B_, C_, H_, W_ = v.shape
        return v.reshape(B_, C_, H_ * W_).transpose(0, 2, 1)

    def _from_tokens(t, like):
        B_, C_, H_, W_ = like.shape
        return t.transpose(0, 2, 1).reshape(B_, C_, H_, W_)
    x = x + _L0_conv_ref(_gn(x), L0_conv_weight, L0_conv_bias_term)
    x = x + _L1_conv_ref(_gn(x), L1_conv_weight_coord, L1_conv_radius, L1_conv_weights)
    return x

_drawn_inputs = setup_inputs


def setup_inputs(seed=0):
    import zlib

    import numpy as np

    out = dict(_drawn_inputs(seed))
    spreads = {'L0_conv_bias_term': (0.0, 2.0), 'L1_conv_radius': (0.3636363744735718, 0.6)}
    factors = {'L1_conv_weight_coord': 43.915, 'L1_conv_weights': 30.854}
    for name, (base, spread) in spreads.items():
        noise = np.random.default_rng([zlib.crc32(name.encode()), seed]).standard_normal(out[name].shape)
        drawn = base * np.exp(spread * noise) if base else spread * noise
        out[name] = jnp.asarray(drawn.astype(out[name].dtype))
    for name, factor in factors.items():
        out[name] = (out[name] * factor).astype(out[name].dtype)
    return out
```

```python
from contextlib import ExitStack

import concourse.bass as bass
from concourse import mybir

ALU = mybir.AluOpType
ACT = mybir.ActivationFunctionType
AX_X = mybir.AxisListType.X
F32 = mybir.dt.float32
F32R = mybir.dt.float32r

P = 128
B, C, H, W = 32, 192, 56, 56
GROUPS = 32
CG = C // GROUPS
BANDS = 4
HB = 16
HB_LAST = H - (BANDS - 1) * HB
RUN = HB * W
HALF = RUN // 2
HALVES = H * W // HALF
M = 2 * H
JW = W // 2
N = JW * B
BANK = 512
JB = JW // 2
CP = 96
CT = C // CP
K1, K2 = 31, 11
POINTS = 4
EPS = 1e-5

X_RING = 4
H_RING = 4
P_RING = 3
T_RING = 2
AHEAD = 2
SLOTS = 2 * CG
NORM_STEPS = 20


class Filter:

    def __init__(self, K):
        self.K = K
        self.pad = K // 2
        self.top = (self.pad + 1) // 2
        self.D = 2 * self.top + 1
        self.half = 2 * self.D
        self.row = 2 * self.half
        self.block = H * self.row
        self.windows = []
        for q in range(BANDS):
            first, last = HB * q, min(H, HB * q + HB) - 1
            self.windows.append((max(0, first - self.pad), min(H - 1, last + self.pad) + 1))
        self.margin = HB - 1
        self.rows = K + 2 * self.margin
        self.padded = self.rows * self.row
        self.pitch = (self.rows - self.margin) * self.row
        self.shifts = [0] + [d for d in range(-self.top, self.top + 1) if d]

    def taps(self, parity_in, parity_out):
        offset = parity_in - parity_out - 1
        first = 0 if offset == 0 else 1
        return 2 * first + offset, first, (self.K - 1 - (2 * first + offset)) // 2 + 1


def job(i, s):
    if isinstance(i, int) and i == 0:
        return s
    if isinstance(i, int) and i == GROUPS:
        return SLOTS * i - SLOTS + s
    return i * SLOTS + (s - CG)


def slots(i):
    if isinstance(i, int) and i == 0:
        return range(CG)
    if isinstance(i, int) and i == GROUPS:
        return range(CG, SLOTS)
    return range(SLOTS)


def ring(i, s, size):
    return job(i if isinstance(i, int) else 1, s) % size


def later(i, s, k):
    s += k
    if isinstance(i, int) and i == 0:
        return (i, s) if s < CG else (1, s - CG)
    if s < SLOTS:
        return i, s
    if isinstance(i, int) and i == GROUPS:
        return None
    if isinstance(i, int) and i == GROUPS - 1:
        return GROUPS, s - SLOTS + CG
    return i + 1, s - SLOTS


def positive(value):
    return not isinstance(value, int) or value > 0


def conv_norm_kernel(nc, x, weight1, bias, coord, radius, weight2, out):
    f1, f2 = Filter(K1), Filter(K2)

    with ExitStack() as ctx:
        def sb(name, shape, dt=F32):
            return ctx.enter_context(nc.sbuf_tensor(name, shape, dt))

        def sem(name):
            return ctx.enter_context(nc.semaphore(name))

        raw = sb("raw", [P, X_RING, CG * RUN])
        xn = sb("xn", [P, RUN])
        xt = sb("xt", [P, 2, N])
        x_hi = sb("x_hi", [P, H_RING, N], F32R)
        x_lo = sb("x_lo", [P, H_RING, N], F32R)
        y = sb("y", [P, RUN])
        toep1 = sb("toep1", [P, T_RING, f1.block], F32R)
        toep2 = sb("toep2", [P, T_RING, f2.block], F32R)
        bias_all = sb("bias_all", [P, C])
        part1 = sb("part1", [P, 2, CG, 6])
        part2 = sb("part2", [P, 2, CG, 6])
        norm1 = sb("norm1", [P, 2])
        norm2 = sb("norm2", [P, 2])
        agg = sb("agg", [P, 2, 2])
        halves = sb("halves", [B, 2, HALVES])
        halves_tmp = sb("halves_tmp", [B, 2, HALVES])
        small = sb("small", [B, 8])
        eps_col = sb("eps_col", [B, 1])

        w1_src = sb("w1_src", [CP, CT, K1 * K1])
        w2_src = sb("w2_src", [CP, CT, POINTS])
        coord_all = sb("coord_all", [CP, POINTS * 2])
        radius_all = sb("radius_all", [CP, POINTS])
        lin = sb("lin", [CP, 2, K2])
        dist = sb("dist", [CP, 2, K2])
        dist_raw = sb("dist_raw", [CP, 2, K2])
        hat = sb("hat", [CP, K2 * K2])
        taps2 = sb("taps2", [CP, CT, K2 * K2])
        pad2_all = sb("pad2_all", [CP, (2 * CT - 1) * f2.pitch + f2.padded])

        acc = ctx.enter_context(nc.psum_tensor("acc", [P, P_RING, 2, BANK], F32))

        padded1 = nc.dram_tensor("padded1", [C, 2, f1.padded], F32)
        padded2 = nc.dram_tensor("padded2", [C, 2, f2.padded], F32)

        x_landed = sem("x_landed")
        w_landed = sem("w_landed")
        toep1_landed = [sem(f"toep1_landed{k}") for k in range(T_RING)]
        toep2_landed = [sem(f"toep2_landed{k}") for k in range(T_RING)]
        bufs_zeroed = sem("bufs_zeroed")
        toep_zeroed = sem("toep_zeroed")
        taps_chain = sem("taps_chain")
        taps2_ready = sem("taps2_ready")
        w_hi_ready = sem("w_hi_ready")
        w_lo_ready = sem("w_lo_ready")
        padded_stored = sem("padded_stored")
        parts1_ready = sem("parts1_ready")
        parts2_ready = sem("parts2_ready")
        norm_chain = sem("norm_chain")
        var_ready = sem("var_ready")
        std_ready = sem("std_ready")
        xn_ready = sem("xn_ready")
        xt_ready = sem("xt_ready")
        hi_ready = sem("hi_ready")
        lo_ready = sem("lo_ready")
        conv_done = sem("conv_done")
        y_ready = sem("y_ready")
        residual_added = sem("residual_added")
        out_stored = sem("out_stored")

        x_dram = x.rearrange("b (g c) h w -> b g c (h w)", c=CG)
        out_dram = out.rearrange("b (g c) h w -> b g c (h w)", c=CG)

        spare = raw[0:CP, 1:X_RING, :].rearrange("p g n -> p (g n)")
        pad1 = [[spare[:, (2 * t + e) * f1.pitch:(2 * t + e) * f1.pitch + f1.padded] for e in range(2)]
                for t in range(CT)]
        pad2 = [[pad2_all[:, (2 * t + e) * f2.pitch:(2 * t + e) * f2.pitch + f2.padded] for e in range(2)]
                for t in range(CT)]

        def padded_taps(tile, f, part, parity_in, parity_out):
            _, first, count = f.taps(parity_in, parity_out)
            rows = tile.rearrange("p (r q e d) -> p r q e d", q=2, e=2, d=f.D)
            return rows[:, f.margin:f.margin + f.K, parity_out, part, first:first + count]

        def plain_taps(tile, f, parity_in, parity_out):
            column, _, count = f.taps(parity_in, parity_out)
            return tile.rearrange("p (h w) -> p h w", w=f.K)[:, ::-1, column:column + 2 * count - 1:2]

        PARITIES = [(e, o) for e in range(2) for o in range(2)]

        def raw_channel(g, c):
            return raw[:, g % X_RING, c * RUN:(c + 1) * RUN]

        def band_rows(q):
            return HB if q < BANDS - 1 else HB_LAST

        def raw_band(g, q, c0, c1):
            return raw[B * q:B * q + B, g % X_RING, c0 * RUN:c1 * RUN].rearrange(
                "p (c n) -> p c n", n=RUN)[:, :, 0:band_rows(q) * W]

        def dram_band(images, g, q, c0, c1):
            return images[:, g, c0:c1, q * RUN:q * RUN + band_rows(q) * W]

        def blocks(tile):
            return tile.rearrange("p (h j e) -> p j h e", h=HB, e=2)

        block = ctx.enter_context(nc.Block())

        @block.sync
        def _(sp):
            def load_x(g):
                for q in range(BANDS):
                    sp.dma_start(raw_band(g, q, 0, CG), dram_band(x_dram, g, q, 0, CG)).then_inc(x_landed, 16)

            def load_toeplitz(m, place, f, padded, toep, landed):
                for q in range(BANDS):
                    (lo, hi), rows = f.windows[q], band_rows(q)
                    first = HB - rows
                    src = bass.AP(padded, m * (2 * f.padded) + (lo - HB * q + f.pad + first) * f.row,
                                  [[f.row, rows], [f.padded, 2], [1, (hi - lo) * f.row]])
                    sp.dma_start(toep[2 * (HB * q + first):2 * HB * (q + 1), place, lo * f.row:hi * f.row].bitcast(F32), src
                                 ).then_inc(landed[place], 16)

            def load_toeplitz1(m, place):
                load_toeplitz(m, place, f1, padded1, toep1, toep1_landed)

            def load_toeplitz2(m, place):
                load_toeplitz(m, place, f2, padded2, toep2, toep2_landed)

            def store(g, c0, c1):
                for q in range(BANDS):
                    sp.dma_start(dram_band(out_dram, g, q, c0, c1), raw_band(g, q, c0, c1)).then_inc(out_stored, 16)

            load_x(0)
            sp.dma_start(w1_src[:], weight1.rearrange("(t p) o h w -> p t (o h w)", p=CP)).then_inc(w_landed, 16)
            sp.dma_start(w2_src[:], weight2.rearrange("o (t p) n -> p t (o n)", p=CP)).then_inc(w_landed, 16)
            sp.dma_start(coord_all[:], coord.rearrange("o n e -> o (n e)").to_broadcast([CP, POINTS * 2])).then_inc(w_landed, 16)
            sp.dma_start(radius_all[:], radius.rearrange("o n a b -> o (n a b)").to_broadcast([CP, POINTS])).then_inc(w_landed, 16)
            sp.dma_start(bias_all[:], bias.rearrange("(o c) -> o c", o=1).to_broadcast([P, C])).then_inc(w_landed, 16)
            sp.wait_ge(w_lo_ready, 4 * 2 * CT)
            for t in range(CT):
                rows = slice(t * CP, (t + 1) * CP)
                for e in range(2):
                    sp.dma_start(padded1[rows, e, :], pad1[t][e]).then_inc(padded_stored, 16)
                    sp.dma_start(padded2[rows, e, :], pad2[t][e]).then_inc(padded_stored, 16)
            sp.wait_ge(padded_stored, 16 * 4 * CT)
            sp.wait_ge(toep_zeroed, 2)
            for m in range(T_RING):
                load_toeplitz1(m, m)
            sp.wait_ge(x_landed, 16 * BANDS)
            load_x(1)
            for m in range(T_RING):
                load_toeplitz2(m, m)

            def iteration(i):
                for s in slots(i):
                    n = job(i, s)
                    if positive(n):
                        sp.wait_ge(conv_done, n)
                    if 1 <= s <= CG and not (isinstance(i, int) and (i == GROUPS or i * CG + s + 1 >= C)):
                        load_toeplitz1(i * CG + (s + 1), (s + 1) % T_RING)
                    if s == 0 and isinstance(i, int) and i == 1:
                        load_toeplitz1(CG + 1, 1)
                    if s == 0 and not (isinstance(i, int) and i < 2):
                        load_toeplitz2(i * CG - (CG - 1), 1)
                    if s > CG and not (isinstance(i, int) and (i - 1) * CG + s - CG + 1 >= C):
                        load_toeplitz2(i * CG + (s - 2 * CG + 1), (s - CG + 1) % T_RING)
                    if s == 1 and not (isinstance(i, int) and i < 2):
                        sp.wait_ge(residual_added, job(i, 0))
                        store(i - 2, CG // 2, CG)
                    if s == 2 and not (isinstance(i, int) and i + 2 >= GROUPS):
                        if positive(i - 1):
                            sp.wait_ge(out_stored, (i - 1) * (16 * BANDS * 2))
                        sp.wait_ge(x_landed, (i + 2) * (16 * BANDS))
                        load_x(i + 2)
                    if s == SLOTS - 2:
                        sp.wait_ge(residual_added, job(i, s - 2) + 1)
                        store(i - 1, 0, CG // 2)

            iteration(0)
            iteration(1)
            with sp.Fori(2, GROUPS - 2) as i:
                iteration(i)
            iteration(GROUPS - 2)
            iteration(GROUPS - 1)
            sp.wait_ge(conv_done, job(GROUPS, CG))
            sp.wait_ge(residual_added, job(GROUPS, CG))
            store(GROUPS - 2, CG // 2, CG)
            load_toeplitz2(C - CG + 1, 1)
            iteration(GROUPS)
            sp.wait_ge(residual_added, SLOTS * GROUPS)
            store(GROUPS - 1, CG // 2, CG)
            sp.wait_ge(out_stored, 16 * BANDS * 2 * GROUPS)

        @block.gpsimd
        def _(pool):
            nc.gpsimd.memset(toep1[:].bitcast(F32), 0.0).then_inc(toep_zeroed, 1)
            nc.gpsimd.memset(toep2[:].bitcast(F32), 0.0).then_inc(toep_zeroed, 1)

        @block.scalar
        def _(act):
            def high_part(i, s):
                n = job(i, s)
                act.wait_ge(xt_ready, n + 1)
                if positive(n - (H_RING - 1)):
                    act.wait_ge(conv_done, n - (H_RING - 1))
                nc.scalar.activation(x_hi[:, ring(i, s, H_RING), :], xt[:, ring(i, s, 2), :], ACT.Copy).then_inc(hi_ready, 1)

            def root(f):
                act.wait_ge(var_ready, f + 1)
                nc.scalar.activation(small[:, 5:6], small[:, 4:5], ACT.Sqrt, bias=eps_col[:]).then_inc(std_ready, 1)

            act.wait_ge(bufs_zeroed, 5)
            act.wait_ge(w_landed, 16 * 5)
            for t in range(CT):
                for e, o in PARITIES:
                    nc.scalar.activation(padded_taps(pad1[t][e].bitcast(F32R), f1, 0, e, o),
                                         plain_taps(w1_src[:, t, :], f1, e, o), ACT.Copy).then_inc(w_hi_ready, 1)
            act.wait_ge(taps2_ready, 1)
            for t in range(CT):
                for e, o in PARITIES:
                    nc.scalar.activation(padded_taps(pad2[t][e].bitcast(F32R), f2, 0, e, o),
                                         plain_taps(taps2[:, t, :], f2, e, o), ACT.Copy).then_inc(w_hi_ready, 1)
            root(0)
            for s in range(AHEAD):
                high_part(0, s)

            def iteration(i):
                for s in slots(i):
                    after = later(i, s, AHEAD)
                    if after:
                        high_part(*after)
                    if isinstance(i, int) and i == 0:
                        if s == CG - 1 - AHEAD:
                            root(1)
                        if s == CG - 1:
                            root(2)
                    elif s == SLOTS - 1 - AHEAD and not (isinstance(i, int) and i == GROUPS):
                        root(i * 2 + 1)
                        if not (isinstance(i, int) and i == GROUPS - 1):
                            root(i * 2 + 2)

            iteration(0)
            with act.Fori(1, GROUPS - 1) as i:
                iteration(i)
            iteration(GROUPS - 1)
            iteration(GROUPS)

        @block.vector
        def _(dve):
            def normalisation(f, g, parts, parts_ready, norm):
                done = [0]

                def link(ins):
                    done[0] += 1
                    ins.then_inc(norm_chain, 1)

                def settle():
                    dve.wait_ge(norm_chain, f * NORM_STEPS + done[0])

                dve.wait_ge(parts_ready, (g + 1) * (2 * CG))
                nc.vector.memset(small[:, 1:2], 0.0)
                link(nc.vector.bn_aggr(agg[:, 0, :], parts[:, 0].rearrange("p c k -> p (c k)")))
                link(nc.vector.bn_aggr(agg[0:B * (BANDS - 1), 1, :],
                                       parts[0:B * (BANDS - 1), 1].rearrange("p c k -> p (c k)")))
                settle()
                for k in range(HALVES):
                    q = k // 2
                    link(nc.vector.tensor_copy(halves[:, :, k], agg[B * q:B * q + B, k % 2, :]))
                settle()
                link(nc.vector.tensor_reduce(small[:, 0:1], halves[:, 0, :], AX_X, ALU.add))
                settle()
                link(nc.vector.tensor_scalar(small[:, 6:7], small[:, 0:1], 1.0 / HALVES, None, ALU.mult))
                settle()
                link(nc.vector.tensor_scalar(halves_tmp[:, 0, :], halves[:, 0, :], small[:, 6:7], None, ALU.subtract))
                settle()
                link(nc.vector.tensor_tensor(halves_tmp[:, 1, :], halves_tmp[:, 0, :], halves_tmp[:, 0, :], ALU.mult))
                settle()
                link(nc.vector.tensor_tensor(halves_tmp[:, 0, :], halves_tmp[:, 1, :], halves[:, 1, :], ALU.add))
                settle()
                link(nc.vector.tensor_reduce(small[:, 3:4], halves_tmp[:, 0, :], AX_X, ALU.add))
                settle()
                nc.vector.tensor_scalar(small[:, 4:5], small[:, 3:4], 1.0 / HALVES, None, ALU.mult).then_inc(var_ready, 1)
                dve.wait_ge(std_ready, f + 1)
                link(nc.vector.reciprocal(small[:, 7:8], small[:, 5:6]))
                settle()
                for q in range(BANDS):
                    link(nc.vector.tensor_copy(norm[B * q:B * q + B, :], small[:, 6:8]))
                settle()
                assert done[0] == NORM_STEPS

            def statistics(parts, parts_ready, g, c):
                for k in range(2):
                    held = P if k == 0 else B * (BANDS - 1)
                    nc.vector.bn_stats(parts[0:held, k, c, :], raw_channel(g, c)[0:held, k * HALF:(k + 1) * HALF]
                                       ).then_inc(parts_ready, 1)

            def prepare(i, s):
                n = job(i, s)
                g, c = (i, s) if s < CG else (i - 1, s - CG)
                norm = norm1 if s < CG else norm2
                if positive(n):
                    dve.wait_ge(xt_ready, n)
                nc.vector.tensor_scalar(xn[:], raw_channel(g, c), norm[:, 0:1], norm[:, 1:2],
                                        ALU.subtract, ALU.mult).then_inc(xn_ready, 1)
                dve.wait_ge(xn_ready, n + 1)
                if positive(n - 1):
                    dve.wait_ge(lo_ready, n - 1)
                nc.vector.transpose(xt[:, ring(i, s, 2), :].rearrange("p (j b) -> p j b", b=B),
                                    blocks(xn[:])[:, :, ::-1, :]).then_inc(xt_ready, 1)

            def low_part(i, s):
                n = job(i, s)
                dve.wait_ge(hi_ready, n + 1)
                nc.vector.tensor_tensor(x_lo[:, ring(i, s, H_RING), :], xt[:, ring(i, s, 2), :],
                                        x_hi[:, ring(i, s, H_RING), :].bitcast(F32), ALU.subtract).then_inc(lo_ready, 1)

            def finish(i, s):
                n = job(i, s)
                g, c = (i, s) if s < CG else (i - 1, s - CG)
                dve.wait_ge(conv_done, n + 1)
                if positive(n):
                    dve.wait_ge(residual_added, n)
                nc.vector.transpose(blocks(y[:]), acc[:, ring(i, s, P_RING), :, 0:N // 2]).then_inc(y_ready, 1)
                dve.wait_ge(y_ready, n + 1)
                if s < CG:
                    nc.vector.scalar_tensor_tensor(raw_channel(g, c), y[:], bias_all[:, bass.ds(g * CG + c, 1)],
                                                   raw_channel(g, c), ALU.add, ALU.add).then_inc(residual_added, 1)
                else:
                    nc.vector.tensor_tensor(raw_channel(g, c), y[:], raw_channel(g, c), ALU.add
                                            ).then_inc(residual_added, 1)

            nc.vector.memset(spare[:, 0:(2 * CT - 1) * f1.pitch + f1.padded], 0.0).then_inc(bufs_zeroed, 1)
            nc.vector.memset(pad2_all[:], 0.0).then_inc(bufs_zeroed, 1)
            nc.vector.memset(raw[B * (BANDS - 1):P].rearrange("p g (c n) -> p (g c) n", n=RUN)[:, :, HALF:RUN], 0.0
                             ).then_inc(bufs_zeroed, 1)
            nc.vector.memset(acc[B * (BANDS - 1):P], 0.0).then_inc(bufs_zeroed, 1)
            nc.vector.memset(eps_col[:], EPS).then_inc(bufs_zeroed, 1)
            dve.wait_ge(bufs_zeroed, 5)

            steps = [0]

            def step(ins):
                steps[0] += 1
                ins.then_inc(taps_chain, 1)
                dve.wait_ge(taps_chain, steps[0])

            for k in range(K2):
                at = -1.0 + 2.0 * k / (K2 - 1)
                nc.vector.memset(lin[:, 0, k:k + 1], at)
                step(nc.vector.memset(lin[:, 1, K2 - 1 - k:K2 - k], at))
            dve.wait_ge(w_landed, 16 * 5)
            step(nc.vector.reciprocal(radius_all[:], radius_all[:]))
            for p in range(POINTS):
                for axis in range(2):
                    step(nc.vector.tensor_scalar(dist_raw[:, axis, :], lin[:, axis, :],
                                                 coord_all[:, 2 * p + axis:2 * p + axis + 1], None, ALU.subtract))
                step(nc.vector.scalar_tensor_tensor(dist[:], dist_raw[:], -1.0, dist_raw[:], ALU.mult, ALU.max))
                grid = hat[:].rearrange("p (h w) -> p h w", w=K2)
                step(nc.vector.tensor_tensor(grid, dist[:, 0, :].unsqueeze(1).to_broadcast([CP, K2, K2]),
                                             dist[:, 1, :].unsqueeze(2).to_broadcast([CP, K2, K2]), ALU.add))
                step(nc.vector.tensor_scalar(hat[:], hat[:], radius_all[:, p:p + 1], -1.0, ALU.mult, ALU.mult))
                step(nc.vector.tensor_scalar(hat[:], hat[:], 1.0, 0.0, ALU.add, ALU.max))
                for t in range(CT):
                    if p == 0:
                        step(nc.vector.tensor_scalar(taps2[:, t, :], hat[:], w2_src[:, t, p:p + 1], None, ALU.mult))
                    else:
                        step(nc.vector.scalar_tensor_tensor(taps2[:, t, :], hat[:], w2_src[:, t, p:p + 1], taps2[:, t, :],
                                                            ALU.mult, ALU.add))
            nc.vector.memset(small[:], 0.0).then_inc(taps2_ready, 1)

            for t in range(CT):
                for k, (e, o) in enumerate(PARITIES):
                    dve.wait_ge(w_hi_ready, 4 * t + k + 1)
                    nc.vector.tensor_tensor(padded_taps(pad1[t][e].bitcast(F32R), f1, 1, e, o),
                                            plain_taps(w1_src[:, t, :], f1, e, o),
                                            padded_taps(pad1[t][e], f1, 0, e, o), ALU.subtract).then_inc(w_lo_ready, 1)
            for t in range(CT):
                for k, (e, o) in enumerate(PARITIES):
                    dve.wait_ge(w_hi_ready, 4 * (CT + t) + k + 1)
                    nc.vector.tensor_tensor(padded_taps(pad2[t][e].bitcast(F32R), f2, 1, e, o),
                                            plain_taps(taps2[:, t, :], f2, e, o),
                                            padded_taps(pad2[t][e], f2, 0, e, o), ALU.subtract).then_inc(w_lo_ready, 1)

            dve.wait_ge(x_landed, 16 * BANDS)
            for c in range(CG):
                statistics(part1, parts1_ready, 0, c)
            normalisation(0, 0, part1, parts1_ready, norm1)
            for s in range(AHEAD):
                prepare(0, s)
                low_part(0, s)

            def iteration(i):
                peeled = isinstance(i, int)
                for s in slots(i):
                    after = later(i, s, AHEAD)
                    if s == 2 and not (peeled and (i == 0 or i >= GROUPS - 1)):
                        dve.wait_ge(x_landed, (i + 2) * (16 * BANDS))
                    if after:
                        prepare(*after)
                    if peeled and i == 0:
                        if s == CG - 1 - AHEAD:
                            dve.wait_ge(x_landed, 16 * BANDS * 2)
                            for c in range(CG):
                                statistics(part1, parts1_ready, 1, c)
                            normalisation(1, 1, part1, parts1_ready, norm1)
                    elif not (peeled and i >= GROUPS - 1):
                        if 2 <= s < 2 + CG:
                            statistics(part1, parts1_ready, i + 1, s - 2)
                    if s == SLOTS - 1 - AHEAD and not (peeled and i == GROUPS):
                        normalisation(i * 2 + 1, i, part2, parts2_ready, norm2)
                        if not (peeled and i == GROUPS - 1):
                            normalisation(i * 2 + 2, i + 1, part1, parts1_ready, norm1)
                    finish(i, s)
                    if s < CG:
                        dve.wait_ge(residual_added, job(i, s) + 1)
                    if after:
                        low_part(*after)
                    if s < CG:
                        statistics(part2, parts2_ready, i, s)
                    if peeled and i == 0 and s == CG - 1:
                        normalisation(2, 0, part2, parts2_ready, norm2)

            iteration(0)
            with dve.Fori(1, GROUPS - 1) as i:
                iteration(i)
            iteration(GROUPS - 1)
            iteration(GROUPS)

        @block.tensor
        def _(pe):
            def toeplitz(toep, f, place, part, d):
                start = place * f.block + part * f.D + d + f.top
                return bass.AP(toep, start, [[T_RING * f.block, P], [f.half, M]])

            def convolve(i, s, f, toep, place):
                h, p = ring(i, s, H_RING), ring(i, s, P_RING)
                for d in f.shifts:
                    for k in range(2):
                        j0, j1 = max(k * JB, -d), min((k + 1) * JB, JW - d)
                        dst = acc[0:M, p, k, (j0 - k * JB) * B:(j1 - k * JB) * B]
                        cols = slice((j0 + d) * B, (j1 + d) * B)
                        for part, src in ((0, x_hi), (0, x_lo), (1, x_hi)):
                            last = nc.tensor.matmul(dst, toeplitz(toep, f, place, part, d), src[:, h, cols],
                                                    start=(d == 0 and part == 0 and src is x_hi),
                                                    stop=(d == f.shifts[-1] and part == 1), skip_group_check=True)
                return last

            def iteration(i):
                for s in slots(i):
                    n = job(i, s)
                    pe.wait_ge(lo_ready, n + 1)
                    if positive(n + 1 - P_RING):
                        pe.wait_ge(y_ready, n + 1 - P_RING)
                    if s < CG:
                        pe.wait_ge(toep1_landed[s % T_RING], i * (16 * BANDS * CG // T_RING) + 16 * BANDS * (s // T_RING + 1))
                        last = convolve(i, s, f1, toep1, s % T_RING)
                    else:
                        c = s - CG
                        pe.wait_ge(toep2_landed[c % T_RING],
                                   (i - 1) * (16 * BANDS * CG // T_RING) + 16 * BANDS * (c // T_RING + 1))
                        last = convolve(i, s, f2, toep2, c % T_RING)
                    last.then_inc(conv_done, 1)

            iteration(0)
            with pe.Fori(1, GROUPS - 1) as i:
                iteration(i)
            iteration(GROUPS - 1)
            iteration(GROUPS)


_INS = ["x", "L0_conv_weight", "L0_conv_bias_term", "L1_conv_weight_coord", "L1_conv_radius", "L1_conv_weights"]


def kernel(**inputs):
    import numpy as _np
    import concourse.bacc as _bacc
    from concourse.bass_utils import run_bass_kernel_spmd as _run

    nc = _bacc.Bacc("TRN2", target_bir_lowering=False, num_devices=1)
    arrays, args = {}, []
    for name in _INS:
        a = _np.ascontiguousarray(inputs[name])
        arrays[f"in_{name}_dram"] = a
        args.append(nc.dram_tensor(f"in_{name}_dram", a.shape, mybir.dt.from_np(a.dtype), kind="ExternalInput").ap())
    out = nc.dram_tensor("out_0_dram", (B, C, H, W), F32, kind="ExternalOutput").ap()
    conv_norm_kernel(nc, *args, out)
    r = _run(nc, [arrays], core_ids=[0])
    return r.results[0]["out_0_dram"]
```

```python
from contextlib import ExitStack

import concourse.bass as bass
from concourse import mybir

ALU = mybir.AluOpType
ACT = mybir.ActivationFunctionType
AX_X = mybir.AxisListType.X
F32 = mybir.dt.float32
F32R = mybir.dt.float32r

P = 128
B, C, H, W = 32, 192, 56, 56
GROUPS = 32
CG = C // GROUPS
BANDS = 4
HB = 16
HB_LAST = H - (BANDS - 1) * HB
RUN = HB * W
HALF = RUN // 2
HALVES = H * W // HALF
M = 2 * H
JW = W // 2
N = JW * B
BANK = 512
JH = JW // 2
N_OP = (2 * JH + JH + 1) * B
CP = 96
CT = C // CP
K1, K2 = 31, 11
POINTS = 4
EPS = 1e-5

X_RING = 4
H_RING = 3
P_RING = 2
T_RING = 2
AHEAD = 2
SLOTS = 2 * CG
NORM_STEPS = 24


class Filter:

    def __init__(self, K):
        self.K = K
        self.pad = K // 2
        self.top = (self.pad + 1) // 2
        self.D = 2 * self.top + 1
        near = range(-self.top - 1, self.top + 1)
        self.evens = [m for m in near if abs(2 * m) <= self.top]
        self.odds = [m for m in near if abs(2 * m + 1) <= self.top]
        self.sums = [m for m in near if m in self.evens or m in self.odds]
        self.base = 2 * self.sums[0]
        self.width = 2 * len(self.sums)
        self.L = self.D + len(self.sums)
        self.half = 2 * self.L
        self.row = 2 * self.half
        self.block = H * self.row
        self.windows = []
        for q in range(BANDS):
            first, last = HB * q, min(H, HB * q + HB) - 1
            self.windows.append((max(0, first - self.pad), min(H - 1, last + self.pad) + 1))
        self.margin = HB - 1
        self.rows = K + 2 * self.margin
        self.padded = self.rows * self.row
        self.pitch = (self.rows - self.margin) * self.row

    def taps(self, parity_in, parity_out):
        column = (parity_in - parity_out + self.pad) % 2
        shift = (column - parity_in + parity_out - self.pad) // 2
        return column, shift - self.base, len(range(column, self.K, 2))

    def products(self):
        return [
            (0, 0, JH, JH + 1, [(m, 2 * m + self.top) for m in self.evens]),
            (JH, 0, JH, JH, [(m, 2 * m + 1 + self.top) for m in self.odds]),
            (2 * JH, -1, JH + 1, JH, [(m, self.D + m - self.sums[0]) for m in self.sums]),
        ]


def job(i, s):
    if isinstance(i, int) and i == 0:
        return s
    if isinstance(i, int) and i == GROUPS:
        return SLOTS * i - SLOTS + s
    return i * SLOTS + (s - CG)


def slots(i):
    if isinstance(i, int) and i == 0:
        return range(CG)
    if isinstance(i, int) and i == GROUPS:
        return range(CG, SLOTS)
    return range(SLOTS)


def ring(i, s, size):
    return job(i if isinstance(i, int) else 1, s) % size


def later(i, s, k):
    s += k
    if isinstance(i, int) and i == 0:
        return (i, s) if s < CG else (1, s - CG)
    if s < SLOTS:
        return i, s
    if isinstance(i, int) and i == GROUPS:
        return None
    if isinstance(i, int) and i == GROUPS - 1:
        return GROUPS, s - SLOTS + CG
    return i + 1, s - SLOTS


def positive(value):
    return not isinstance(value, int) or value > 0


def conv_norm_kernel(nc, x, weight1, bias, coord, radius, weight2, out):
    f1, f2 = Filter(K1), Filter(K2)

    with ExitStack() as ctx:
        def sb(name, shape, dt=F32):
            return ctx.enter_context(nc.sbuf_tensor(name, shape, dt))

        def sem(name):
            return ctx.enter_context(nc.semaphore(name))

        raw = sb("raw", [P, X_RING, CG * RUN])
        scratch = sb("scratch", [P, RUN])
        xt = sb("xt", [P, B + N + B])
        xs = sb("xs", [P, (JH + 1) * B])
        x_hi = sb("x_hi", [P, H_RING, N_OP], F32R)
        x_lo = sb("x_lo", [P, H_RING, N_OP], F32R)
        p0 = sb("p0", [P, (JH + 1) * B])
        p1 = sb("p1", [P, JH * B])
        yt = sb("yt", [P, N])
        toep1 = sb("toep1", [P, T_RING, f1.block], F32R)
        toep2 = sb("toep2", [P, T_RING, f2.block], F32R)
        bias_all = sb("bias_all", [P, C])
        part1 = sb("part1", [P, 2, CG, 6])
        part2 = sb("part2", [P, 2, CG, 6])
        norm1 = sb("norm1", [P, 2])
        norm2 = sb("norm2", [P, 2])
        agg = sb("agg", [P, 2, 2])
        halves = sb("halves", [B, 2, HALVES])
        halves_tmp = sb("halves_tmp", [B, 2, HALVES])
        small = sb("small", [B, 8])

        w2_src = sb("w2_src", [CP, CT, POINTS])
        coord_all = sb("coord_all", [CP, POINTS * 2])
        radius_all = sb("radius_all", [CP, POINTS])
        lin = sb("lin", [CP, 2, K2])
        dist = sb("dist", [CP, 2, K2])
        dist_raw = sb("dist_raw", [CP, 2, K2])
        hat = sb("hat", [CP, K2 * K2])
        taps2 = sb("taps2", [CP, CT, K2 * K2])

        acc = ctx.enter_context(nc.psum_tensor("acc", [P, P_RING, 3, BANK], F32))

        padded1 = nc.dram_tensor("padded1", [C, 2, f1.padded], F32)
        padded2 = nc.dram_tensor("padded2", [C, 2, f2.padded], F32)

        x_landed = sem("x_landed")
        w_landed = sem("w_landed")
        params_landed = sem("params_landed")
        toep1_landed = [sem(f"toep1_landed{k}") for k in range(T_RING)]
        toep2_landed = [sem(f"toep2_landed{k}") for k in range(T_RING)]
        bufs_zeroed = sem("bufs_zeroed")
        toep_zeroed = sem("toep_zeroed")
        taps_chain = sem("taps_chain")
        taps_laid = sem("taps_laid")
        w_hi_ready = sem("w_hi_ready")
        w_lo_ready = sem("w_lo_ready")
        padded_stored = sem("padded_stored")
        parts1_ready = sem("parts1_ready")
        parts2_ready = sem("parts2_ready")
        norm_chain = sem("norm_chain")
        var_ready = sem("var_ready")
        std_ready = sem("std_ready")
        xn_ready = sem("xn_ready")
        xt_ready = sem("xt_ready")
        xs_ready = sem("xs_ready")
        hi_ready = sem("hi_ready")
        lo_ready = sem("lo_ready")
        lo_sums_ready = sem("lo_sums_ready")
        conv_done = sem("conv_done")
        p01_done = sem("p01_done")
        p01_copied = sem("p01_copied")
        even_ready = sem("even_ready")
        odd_rest_ready = sem("odd_rest_ready")
        odd_ready = sem("odd_ready")
        y_ready = sem("y_ready")
        residual_added = sem("residual_added")
        out_stored = sem("out_stored")

        x_dram = x.rearrange("b (g c) h w -> b g c (h w)", c=CG)
        out_dram = out.rearrange("b (g c) h w -> b g c (h w)", c=CG)

        spare = raw[0:CP, 1:X_RING, :].rearrange("p g n -> p (g n)")
        area_size = f1.pitch + f1.padded
        area = spare[:, 0:area_size]
        w1_src = spare[:, area_size:area_size + CT * K1 * K1].rearrange("p (t n) -> p t n", t=CT)
        work_start = area_size + CT * K1 * K1
        work_size = K1 * 2 * f1.width

        def work(f, e):
            start = work_start + e * work_size
            return spare[:, start:start + f.K * 2 * f.width].rearrange("p (k o d) -> p k o d", o=2, d=f.width)

        def work_sums(f):
            start = work_start + 2 * work_size
            return spare[:, start:start + f.K * f.width].rearrange("p (k o d) -> p k o d", o=2, d=f.width // 2)

        def padded(f, place):
            return area[:, place * f.pitch:place * f.pitch + f.padded]

        def padded_rows(f, place, part):
            rows = padded(f, place).rearrange("p (r o e m) -> p r o e m", o=2, e=2, m=f.L)
            return rows[:, f.margin:f.margin + f.K, :, part, :]

        STAGES = [[(f1, 0, 0)], [(f1, 1, 0)], [(f2, 0, 0), (f2, 1, 2)]]
        LAID = [2 * sum(len(x) for x in STAGES[:k + 1]) for k in range(len(STAGES))]

        def x0_x1(tile):
            return tile.rearrange("p (j s b) -> p s j b", s=2, b=B)

        def apart(tile):
            return tile[:, 0:N].rearrange("p (s j b) -> p s j b", s=2, b=B)

        def raw_channel(g, c):
            return raw[:, g % X_RING, c * RUN:(c + 1) * RUN]

        def band_rows(q):
            return HB if q < BANDS - 1 else HB_LAST

        def raw_band(g, q, c0, c1):
            return raw[B * q:B * q + B, g % X_RING, c0 * RUN:c1 * RUN].rearrange(
                "p (c n) -> p c n", n=RUN)[:, :, 0:band_rows(q) * W]

        def dram_band(images, g, q, c0, c1):
            return images[:, g, c0:c1, q * RUN:q * RUN + band_rows(q) * W]

        def blocks(tile):
            return tile.rearrange("p (h j e) -> p j h e", h=HB, e=2)

        block = ctx.enter_context(nc.Block())

        @block.sync
        def _(sp):
            def load_x(g):
                for q in range(BANDS):
                    sp.dma_start(raw_band(g, q, 0, CG), dram_band(x_dram, g, q, 0, CG)).then_inc(x_landed, 16)

            def load_toeplitz(m, place, f, padded, toep, landed):
                for q in range(BANDS):
                    (lo, hi), rows = f.windows[q], band_rows(q)
                    first = HB - rows
                    src = bass.AP(padded, m * (2 * f.padded) + (lo - HB * q + f.pad + first) * f.row,
                                  [[f.row, rows], [f.padded, 2], [1, (hi - lo) * f.row]])
                    sp.dma_start(toep[2 * (HB * q + first):2 * HB * (q + 1), place, lo * f.row:hi * f.row].bitcast(F32), src
                                 ).then_inc(landed[place], 16)

            def load_toeplitz1(m, place):
                load_toeplitz(m, place, f1, padded1, toep1, toep1_landed)

            def load_toeplitz2(m, place):
                load_toeplitz(m, place, f2, padded2, toep2, toep2_landed)

            def store(g, c0, c1):
                for q in range(BANDS):
                    sp.dma_start(dram_band(out_dram, g, q, c0, c1), raw_band(g, q, c0, c1)).then_inc(out_stored, 16)

            sp.dma_start(w1_src, weight1.rearrange("(t p) o h w -> p t (o h w)", p=CP)).then_inc(w_landed, 16)
            load_x(0)
            sp.dma_start(w2_src[:], weight2.rearrange("o (t p) n -> p t (o n)", p=CP)).then_inc(params_landed, 16)
            sp.dma_start(coord_all[:], coord.rearrange("o n e -> o (n e)").to_broadcast([CP, POINTS * 2])).then_inc(params_landed, 16)
            sp.dma_start(radius_all[:], radius.rearrange("o n a b -> o (n a b)").to_broadcast([CP, POINTS])).then_inc(params_landed, 16)
            sp.dma_start(bias_all[:], bias.rearrange("(o c) -> o c", o=1).to_broadcast([P, C])).then_inc(params_landed, 16)

            def store_filters(k):
                sp.wait_ge(w_lo_ready, 2 * LAID[k])
                for f, t, place in STAGES[k]:
                    target = padded1 if f is f1 else padded2
                    for e in range(2):
                        sp.dma_start(target[t * CP:(t + 1) * CP, e, :], padded(f, place + e)).then_inc(padded_stored, 16)
                sp.wait_ge(padded_stored, 16 * LAID[k])

            store_filters(0)
            sp.wait_ge(toep_zeroed, 2)
            for m in range(T_RING):
                load_toeplitz1(m, m)

            def iteration(i):
                for s in slots(i):
                    n = job(i, s)
                    if positive(n):
                        sp.wait_ge(conv_done, n)
                    if 1 <= s <= CG and not (isinstance(i, int) and (i == GROUPS or i * CG + s + 1 >= C)):
                        load_toeplitz1(i * CG + (s + 1), (s + 1) % T_RING)
                    if isinstance(i, int) and i == 0 and s in (1, 2):
                        store_filters(s)
                        if s == 2:
                            sp.wait_ge(x_landed, 16 * BANDS)
                            load_x(1)
                            for m in range(T_RING):
                                load_toeplitz2(m, m)
                            continue
                    if s == 0 and isinstance(i, int) and i == 1:
                        load_toeplitz1(CG + 1, 1)
                    if s == 0 and not (isinstance(i, int) and i < 2):
                        load_toeplitz2(i * CG - (CG - 1), 1)
                    if s > CG and not (isinstance(i, int) and (i - 1) * CG + s - CG + 1 >= C):
                        load_toeplitz2(i * CG + (s - 2 * CG + 1), (s - CG + 1) % T_RING)
                    if s == 1 and not (isinstance(i, int) and i < 2):
                        sp.wait_ge(residual_added, job(i, 0))
                        store(i - 2, CG // 2, CG)
                    if s == (4 if isinstance(i, int) and i == 0 else 2) and not (isinstance(i, int) and i + 2 >= GROUPS):
                        if positive(i - 1):
                            sp.wait_ge(out_stored, (i - 1) * (16 * BANDS * 2))
                        sp.wait_ge(x_landed, (i + 2) * (16 * BANDS))
                        load_x(i + 2)
                    if s == SLOTS - 2:
                        sp.wait_ge(residual_added, job(i, s - 2) + 1)
                        store(i - 1, 0, CG // 2)

            iteration(0)
            iteration(1)
            with sp.Fori(2, GROUPS - 2) as i:
                iteration(i)
            iteration(GROUPS - 2)
            iteration(GROUPS - 1)
            sp.wait_ge(conv_done, job(GROUPS, CG))
            sp.wait_ge(residual_added, job(GROUPS, CG))
            store(GROUPS - 2, CG // 2, CG)
            load_toeplitz2(C - CG + 1, 1)
            iteration(GROUPS)
            sp.wait_ge(residual_added, SLOTS * GROUPS)
            store(GROUPS - 1, CG // 2, CG)
            sp.wait_ge(out_stored, 16 * BANDS * 2 * GROUPS)

        @block.gpsimd
        def _(pool):
            nc.gpsimd.memset(toep1[:].bitcast(F32), 0.0).then_inc(toep_zeroed, 1)
            nc.gpsimd.memset(toep2[:].bitcast(F32), 0.0).then_inc(toep_zeroed, 1)

            def combine(i, s):
                n = job(i, s)
                pool.wait_ge(p01_copied, n * 2 + 2)
                if positive(n):
                    pool.wait_ge(y_ready, n)
                nc.gpsimd.tensor_tensor(x0_x1(yt[:])[:, 0], p0[:, 0:JH * B].rearrange("p (j b) -> p j b", b=B),
                                        p1[:].rearrange("p (j b) -> p j b", b=B), ALU.add).then_inc(even_ready, 1)
                pool.wait_ge(even_ready, n + 1)
                nc.gpsimd.tensor_tensor(p1[:], p0[:, B:(JH + 1) * B], p1[:], ALU.add).then_inc(odd_rest_ready, 1)

            def add_pairs(i, s):
                n = job(i, s)
                pool.wait_ge(xt_ready, n + 1)
                if positive(n):
                    pool.wait_ge(lo_sums_ready, n)
                pairs = xt[:].rearrange("p (j s b) -> p s j b", s=2, b=B)
                nc.gpsimd.tensor_tensor(xs[:].rearrange("p (j b) -> p j b", b=B), pairs[:, 0], pairs[:, 1], ALU.add
                                        ).then_inc(xs_ready, 1)

            def low_sums(i, s):
                n = job(i, s)
                h = ring(i, s, H_RING)
                pool.wait_ge(hi_ready, n * 2 + 2)
                nc.gpsimd.tensor_tensor(x_lo[:, h, N:N_OP], xs[:], x_hi[:, h, N:N_OP].bitcast(F32), ALU.subtract
                                        ).then_inc(lo_sums_ready, 1)

            for s in range(AHEAD):
                add_pairs(0, s)
                low_sums(0, s)

            def iteration(i):
                for s in slots(i):
                    combine(i, s)
                    after = later(i, s, AHEAD)
                    if after:
                        add_pairs(*after)
                        low_sums(*after)

            iteration(0)
            with pool.Fori(1, GROUPS - 1) as i:
                iteration(i)
            iteration(GROUPS - 1)
            iteration(GROUPS)

        @block.scalar
        def _(act):
            def high_part(i, s):
                n = job(i, s)
                act.wait_ge(xt_ready, n + 1)
                if positive(n - (H_RING - 1)):
                    act.wait_ge(conv_done, n - (H_RING - 1))
                h = ring(i, s, H_RING)
                nc.scalar.activation(apart(x_hi[:, h, :]), x0_x1(xt[:, B:B + N]), ACT.Copy).then_inc(hi_ready, 1)
                act.wait_ge(xs_ready, n + 1)
                nc.scalar.activation(x_hi[:, h, N:N_OP], xs[:], ACT.Copy).then_inc(hi_ready, 1)

            def copy_products(i, s):
                n = job(i, s)
                act.wait_ge(p01_done, n + 1)
                if positive(n):
                    act.wait_ge(odd_ready, n)
                acc_n = acc[:, ring(i, s, P_RING)]
                nc.scalar.activation(p0[:], acc_n[:, 0, 0:(JH + 1) * B], ACT.Copy).then_inc(p01_copied, 1)
                nc.scalar.activation(p1[:], acc_n[:, 1, 0:JH * B], ACT.Copy).then_inc(p01_copied, 1)

            def root(f):
                act.wait_ge(var_ready, f + 1)
                nc.scalar.activation(small[:, 5:6], small[:, 4:5], ACT.Sqrt).then_inc(std_ready, 1)

            def filters_high(k):
                done = LAID[k] - 2 * len(STAGES[k])
                if k > 0:
                    act.wait_ge(padded_stored, 16 * done)
                for f, t, place in STAGES[k]:
                    for e in range(2):
                        done += 1
                        act.wait_ge(taps_laid, done)
                        dst = padded_rows(f, place + e, 0).bitcast(F32R)
                        first = -f.top - f.base
                        nc.scalar.activation(dst[:, :, :, 0:f.D], work(f, e)[:, :, :, first:first + f.D], ACT.Copy
                                             ).then_inc(w_hi_ready, 1)
                        nc.scalar.activation(dst[:, :, :, f.D:f.L], work_sums(f), ACT.Copy).then_inc(w_hi_ready, 1)

            filters_high(0)
            root(0)
            for s in range(AHEAD):
                high_part(0, s)

            def iteration(i):
                peeled = isinstance(i, int)
                for s in slots(i):
                    if s == 0 and not (peeled and i == 0):
                        root(i * 2)
                    if s == CG - 1 and not (peeled and (i == 0 or i == GROUPS - 1)):
                        root(i * 2 + 1)
                    copy_products(i, s)
                    after = later(i, s, AHEAD)
                    if after:
                        high_part(*after)
                    if peeled and i == 0 and s == CG - 1 - AHEAD:
                        root(1)
                    if peeled and i == GROUPS - 1 and s == SLOTS - 1 - AHEAD:
                        root(2 * GROUPS - 1)
                    if peeled and i == 0 and s in (0, 1):
                        filters_high(s + 1)

            iteration(0)
            with act.Fori(1, GROUPS - 1) as i:
                iteration(i)
            iteration(GROUPS - 1)
            iteration(GROUPS)

        @block.vector
        def _(dve):
            def normalisation(f, g, parts, parts_ready, norm):
                done = [0]

                def link(ins):
                    done[0] += 1
                    ins.then_inc(norm_chain, 1)

                def settle():
                    dve.wait_ge(norm_chain, f * NORM_STEPS + done[0])

                dve.wait_ge(parts_ready, (g + 1) * (2 * CG))
                nc.vector.memset(small[:, 1:2], 0.0)
                link(nc.vector.bn_aggr(agg[:, 0, :], parts[:, 0].rearrange("p c k -> p (c k)")))
                link(nc.vector.bn_aggr(agg[0:B * (BANDS - 1), 1, :],
                                       parts[0:B * (BANDS - 1), 1].rearrange("p c k -> p (c k)")))
                settle()
                for k in range(HALVES):
                    q = k // 2
                    link(nc.vector.tensor_copy(halves[:, :, k], agg[B * q:B * q + B, k % 2, :]))
                settle()
                link(nc.vector.tensor_reduce(small[:, 0:1], halves[:, 0, :], AX_X, ALU.add))
                settle()
                link(nc.vector.tensor_scalar(small[:, 6:7], small[:, 0:1], 1.0 / HALVES, None, ALU.mult))
                settle()
                link(nc.vector.tensor_scalar(halves_tmp[:, 0, :], halves[:, 0, :], small[:, 6:7], None, ALU.subtract))
                settle()
                link(nc.vector.tensor_tensor(halves_tmp[:, 1, :], halves_tmp[:, 0, :], halves_tmp[:, 0, :], ALU.mult))
                settle()
                link(nc.vector.tensor_tensor(halves_tmp[:, 0, :], halves_tmp[:, 1, :], halves[:, 1, :], ALU.add))
                settle()
                link(nc.vector.tensor_reduce(small[:, 3:4], halves_tmp[:, 0, :], AX_X, ALU.add))
                settle()
                nc.vector.tensor_scalar(small[:, 4:5], small[:, 3:4], 1.0 / HALVES, EPS, ALU.mult, ALU.add).then_inc(var_ready, 1)
                dve.wait_ge(std_ready, f + 1)
                link(nc.vector.reciprocal(small[:, 7:8], small[:, 5:6]))
                settle()
                link(nc.vector.tensor_tensor(small[:, 0:1], small[:, 7:8], small[:, 7:8], ALU.mult))
                settle()
                link(nc.vector.tensor_tensor(small[:, 3:4], small[:, 0:1], small[:, 4:5], ALU.mult))
                settle()
                link(nc.vector.tensor_scalar(small[:, 0:1], small[:, 3:4], -0.5, 1.5, ALU.mult, ALU.add))
                settle()
                link(nc.vector.tensor_tensor(small[:, 7:8], small[:, 7:8], small[:, 0:1], ALU.mult))
                settle()
                for q in range(BANDS):
                    link(nc.vector.tensor_copy(norm[B * q:B * q + B, :], small[:, 6:8]))
                settle()
                assert done[0] == NORM_STEPS

            def statistics(parts, parts_ready, g, c):
                for k in range(2):
                    held = P if k == 0 else B * (BANDS - 1)
                    nc.vector.bn_stats(parts[0:held, k, c, :], raw_channel(g, c)[0:held, k * HALF:(k + 1) * HALF]
                                       ).then_inc(parts_ready, 1)

            def prepare(i, s):
                n = job(i, s)
                g, c = (i, s) if s < CG else (i - 1, s - CG)
                norm = norm1 if s < CG else norm2
                if positive(n):
                    dve.wait_ge(xt_ready, n)
                if positive(n - AHEAD):
                    dve.wait_ge(residual_added, n - AHEAD)
                nc.vector.tensor_scalar(scratch[:], raw_channel(g, c), norm[:, 0:1], norm[:, 1:2],
                                        ALU.subtract, ALU.mult).then_inc(xn_ready, 1)
                dve.wait_ge(xn_ready, n + 1)
                if positive(n):
                    dve.wait_ge(lo_ready, n)
                    dve.wait_ge(xs_ready, n)
                nc.vector.transpose(xt[:, B:B + N].rearrange("p (j b) -> p j b", b=B),
                                    blocks(scratch[:])[:, :, ::-1, :]).then_inc(xt_ready, 1)

            def low_part(i, s):
                n = job(i, s)
                h = ring(i, s, H_RING)
                dve.wait_ge(hi_ready, n * 2 + 1)
                nc.vector.tensor_tensor(apart(x_lo[:, h, :]), x0_x1(xt[:, B:B + N]),
                                        apart(x_hi[:, h, :].bitcast(F32)), ALU.subtract).then_inc(lo_ready, 1)

            def finish(i, s, prepared):
                n = job(i, s)
                g, c = (i, s) if s < CG else (i - 1, s - CG)
                dve.wait_ge(conv_done, n + 1)
                dve.wait_ge(odd_rest_ready, n + 1)
                nc.vector.tensor_tensor(x0_x1(yt[:])[:, 1],
                                        acc[:, ring(i, s, P_RING), 2, 0:JH * B].rearrange("p (j b) -> p j b", b=B),
                                        p1[:].rearrange("p (j b) -> p j b", b=B), ALU.subtract).then_inc(odd_ready, 1)
                dve.wait_ge(odd_ready, n + 1)
                dve.wait_ge(xt_ready, prepared)
                if positive(n):
                    dve.wait_ge(residual_added, n)
                nc.vector.transpose(blocks(scratch[:]), yt[:].rearrange("p (j b) -> p j b", b=B)).then_inc(y_ready, 1)
                dve.wait_ge(y_ready, n + 1)
                if s < CG:
                    nc.vector.scalar_tensor_tensor(raw_channel(g, c), scratch[:], bias_all[:, bass.ds(g * CG + c, 1)],
                                                   raw_channel(g, c), ALU.add, ALU.add).then_inc(residual_added, 1)
                else:
                    nc.vector.tensor_tensor(raw_channel(g, c), scratch[:], raw_channel(g, c), ALU.add
                                            ).then_inc(residual_added, 1)

            nc.vector.memset(area, 0.0).then_inc(bufs_zeroed, 1)
            nc.vector.memset(spare[:, work_start:work_start + 2 * work_size], 0.0).then_inc(bufs_zeroed, 1)
            nc.vector.memset(xt[:, 0:B], 0.0).then_inc(bufs_zeroed, 1)
            nc.vector.memset(xt[:, B + N:], 0.0).then_inc(bufs_zeroed, 1)
            nc.vector.memset(raw[B * (BANDS - 1):P].rearrange("p g (c n) -> p (g c) n", n=RUN)[:, :, HALF:RUN], 0.0
                             ).then_inc(bufs_zeroed, 1)
            nc.vector.memset(acc[B * (BANDS - 1):P], 0.0).then_inc(bufs_zeroed, 1)
            dve.wait_ge(bufs_zeroed, 6)

            steps = [0]

            def step(ins):
                steps[0] += 1
                ins.then_inc(taps_chain, 1)
                dve.wait_ge(taps_chain, steps[0])

            def taps_11x11():
                for k in range(K2):
                    at = -1.0 + 2.0 * k / (K2 - 1)
                    nc.vector.memset(lin[:, 0, k:k + 1], at)
                    step(nc.vector.memset(lin[:, 1, K2 - 1 - k:K2 - k], at))
                dve.wait_ge(params_landed, 16 * 4)
                step(nc.vector.reciprocal(radius_all[:], radius_all[:]))
                for p in range(POINTS):
                    for axis in range(2):
                        step(nc.vector.tensor_scalar(dist_raw[:, axis, :], lin[:, axis, :],
                                                     coord_all[:, 2 * p + axis:2 * p + axis + 1], None, ALU.subtract))
                    step(nc.vector.scalar_tensor_tensor(dist[:], dist_raw[:], -1.0, dist_raw[:], ALU.mult, ALU.max))
                    grid = hat[:].rearrange("p (h w) -> p h w", w=K2)
                    step(nc.vector.tensor_tensor(grid, dist[:, 0, :].unsqueeze(1).to_broadcast([CP, K2, K2]),
                                                 dist[:, 1, :].unsqueeze(2).to_broadcast([CP, K2, K2]), ALU.add))
                    step(nc.vector.tensor_scalar(hat[:], hat[:], radius_all[:, p:p + 1], -1.0, ALU.mult, ALU.mult))
                    step(nc.vector.tensor_scalar(hat[:], hat[:], 1.0, 0.0, ALU.add, ALU.max))
                    for t in range(CT):
                        if p == 0:
                            step(nc.vector.tensor_scalar(taps2[:, t, :], hat[:], w2_src[:, t, p:p + 1], None, ALU.mult))
                        else:
                            step(nc.vector.scalar_tensor_tensor(taps2[:, t, :], hat[:], w2_src[:, t, p:p + 1], taps2[:, t, :],
                                                                ALU.mult, ALU.add))

            def filters_low(k):
                done = LAID[k] - 2 * len(STAGES[k])
                if k > 0:
                    dve.wait_ge(padded_stored, 16 * done)
                if k == 2:
                    step(nc.vector.memset(area[:, 0:3 * f2.pitch + f2.padded], 0.0))
                    step(nc.vector.memset(spare[:, work_start:work_start + 2 * work_size], 0.0))
                for f, t, place in STAGES[k]:
                    taps = (w1_src if f is f1 else taps2)[:, t, :].rearrange("p (h w) -> p h w", w=f.K)
                    for e in range(2):
                        done += 1
                        for o in range(2):
                            column, first, count = f.taps(e, o)
                            step(nc.vector.tensor_copy(work(f, e)[:, :, o, first:first + count],
                                                       taps[:, ::-1, column:column + 2 * count - 1:2]))
                        pairs = work(f, e).rearrange("p k o (m s) -> p k o s m", s=2)
                        for o in range(2):
                            step(nc.vector.tensor_tensor(work_sums(f)[:, :, o, :], pairs[:, :, o, 0, :],
                                                         pairs[:, :, o, 1, :], ALU.add))
                        nc.vector.memset(small[:, 2:3], 0.0).then_inc(taps_laid, 1)
                        dve.wait_ge(w_hi_ready, 2 * done)
                        low, high = padded_rows(f, place + e, 1).bitcast(F32R), padded_rows(f, place + e, 0)
                        first = -f.top - f.base
                        nc.vector.tensor_tensor(low[:, :, :, 0:f.D], work(f, e)[:, :, :, first:first + f.D],
                                                high[:, :, :, 0:f.D], ALU.subtract).then_inc(w_lo_ready, 1)
                        nc.vector.tensor_tensor(low[:, :, :, f.D:f.L], work_sums(f), high[:, :, :, f.D:f.L], ALU.subtract
                                                ).then_inc(w_lo_ready, 1)
                        dve.wait_ge(w_lo_ready, 2 * done)

            dve.wait_ge(w_landed, 16)
            filters_low(0)

            dve.wait_ge(x_landed, 16 * BANDS)
            for c in range(CG):
                statistics(part1, parts1_ready, 0, c)
            normalisation(0, 0, part1, parts1_ready, norm1)
            for s in range(AHEAD):
                prepare(0, s)
                low_part(0, s)
            taps_11x11()

            def iteration(i):
                peeled = isinstance(i, int)
                for s in slots(i):
                    after = later(i, s, AHEAD)
                    if s == 0 and not (peeled and (i == 0 or i >= GROUPS - 1)):
                        dve.wait_ge(x_landed, (i + 2) * (16 * BANDS))
                    if after:
                        prepare(*after)
                    if s == 0 and not (peeled and i == 0):
                        normalisation(i * 2, i - 1, part2, parts2_ready, norm2)
                    if peeled and i == 0:
                        if s == CG - 1 - AHEAD:
                            dve.wait_ge(x_landed, 16 * BANDS * 2)
                            for c in range(CG):
                                statistics(part1, parts1_ready, 1, c)
                            normalisation(1, 1, part1, parts1_ready, norm1)
                    elif not (peeled and i >= GROUPS - 1):
                        if s < CG:
                            statistics(part1, parts1_ready, i + 1, s)
                        if s == CG - 1:
                            normalisation(i * 2 + 1, i + 1, part1, parts1_ready, norm1)
                    if peeled and i == GROUPS - 1 and s == SLOTS - 1 - AHEAD:
                        normalisation(2 * GROUPS - 1, i, part2, parts2_ready, norm2)
                    n = job(i, s)
                    finish(i, s, min(n + 1 + AHEAD, SLOTS * GROUPS) if isinstance(n, int) else n + (1 + AHEAD))
                    if s < CG:
                        dve.wait_ge(residual_added, job(i, s) + 1)
                    if after:
                        low_part(*after)
                    if s < CG:
                        statistics(part2, parts2_ready, i, s)
                    if peeled and i == 0 and s in (0, 1):
                        filters_low(s + 1)

            iteration(0)
            with dve.Fori(1, GROUPS - 1) as i:
                iteration(i)
            iteration(GROUPS - 1)
            iteration(GROUPS)

        @block.tensor
        def _(pe):
            def toeplitz(toep, f, place, part, k):
                return bass.AP(toep, place * f.block + part * f.L + k, [[T_RING * f.block, P], [f.half, M]])

            def convolve(i, s, f, toep, place):
                h, p = ring(i, s, H_RING), ring(i, s, P_RING)
                for bank, (start, j_in, n_in, n_out, matrices) in enumerate(f.products()):
                    if bank == 2:
                        pe.wait_ge(lo_sums_ready, job(i, s) + 1)
                    matrices = sorted(matrices, key=lambda x: abs(x[0]))
                    for m, k in matrices:
                        j0, j1 = max(0, j_in - m), min(n_out, j_in + n_in - m)
                        dst = acc[0:M, p, bank, j0 * B:j1 * B]
                        cols = slice((start + j0 + m - j_in) * B, (start + j1 + m - j_in) * B)
                        for part, src in ((0, x_hi), (0, x_lo), (1, x_hi)):
                            last = nc.tensor.matmul(dst, toeplitz(toep, f, place, part, k), src[:, h, cols],
                                                    start=(m == 0 and part == 0 and src is x_hi),
                                                    stop=(m == matrices[-1][0] and part == 1), skip_group_check=True)
                    if bank == 1:
                        last.then_inc(p01_done, 1)
                return last

            def iteration(i):
                for s in slots(i):
                    n = job(i, s)
                    pe.wait_ge(lo_ready, n + 1)
                    if positive(n + 1 - P_RING):
                        pe.wait_ge(odd_ready, n + 1 - P_RING)
                    if s < CG:
                        pe.wait_ge(toep1_landed[s % T_RING], i * (16 * BANDS * CG // T_RING) + 16 * BANDS * (s // T_RING + 1))
                        last = convolve(i, s, f1, toep1, s % T_RING)
                    else:
                        c = s - CG
                        pe.wait_ge(toep2_landed[c % T_RING],
                                   (i - 1) * (16 * BANDS * CG // T_RING) + 16 * BANDS * (c // T_RING + 1))
                        last = convolve(i, s, f2, toep2, c % T_RING)
                    last.then_inc(conv_done, 1)

            iteration(0)
            with pe.Fori(1, GROUPS - 1) as i:
                iteration(i)
            iteration(GROUPS - 1)
            iteration(GROUPS)


_INS = ["x", "L0_conv_weight", "L0_conv_bias_term", "L1_conv_weight_coord", "L1_conv_radius", "L1_conv_weights"]


def kernel(**inputs):
    import numpy as _np
    import concourse.bacc as _bacc
    from concourse.bass_utils import run_bass_kernel_spmd as _run

    nc = _bacc.Bacc("TRN2", target_bir_lowering=False, num_devices=1)
    arrays, args = {}, []
    for name in _INS:
        a = _np.ascontiguousarray(inputs[name])
        arrays[f"in_{name}_dram"] = a
        args.append(nc.dram_tensor(f"in_{name}_dram", a.shape, mybir.dt.from_np(a.dtype), kind="ExternalInput").ap())
    out = nc.dram_tensor("out_0_dram", (B, C, H, W), F32, kind="ExternalOutput").ap()
    conv_norm_kernel(nc, *args, out)
    r = _run(nc, [arrays], core_ids=[0])
    return r.results[0]["out_0_dram"]
```

```python
from contextlib import ExitStack

import concourse.bass as bass
from concourse import mybir

ALU = mybir.AluOpType
ACT = mybir.ActivationFunctionType
AX_X = mybir.AxisListType.X
F32 = mybir.dt.float32
F32R = mybir.dt.float32r

P = 128
B, C, H, W = 32, 192, 56, 56
GROUPS = 32
CG = C // GROUPS
BANDS = 4
HB = 16
HB_LAST = H - (BANDS - 1) * HB
RUN = HB * W
HALF = RUN // 2
HALVES = H * W // HALF
M = 2 * H
JW = W // 2
N = JW * B
BANK = 512
JH = JW // 2
WP = W + 2
JE = JH + 1
N_X = 2 * JE * B
N_OP = N_X + JE * B
CP = 96
CT = C // CP
K1, K2 = 31, 11
POINTS = 4
EPS = 1e-5

X_RING = 4
H_RING = 3
P_RING = 2
T_RING = 2
AHEAD = 2
FIRST, SECOND = 1, 2
PATTERN = ([(FIRST, 0), (FIRST, 1)] + [x for c in range(CG - 2) for x in ((SECOND, c), (FIRST, c + 2))]
           + [(SECOND, CG - 2), (SECOND, CG - 1)])
SLOTS = len(PATTERN)
FIRST_SLOTS = [s for s in range(SLOTS) if PATTERN[s][0] == FIRST]
SECOND_SLOTS = [s for s in range(SLOTS) if PATTERN[s][0] == SECOND]
NORM_STEPS = 24


class Filter:

    def __init__(self, K, first_pair):
        self.K = K
        self.pad = K // 2
        self.first_pair = first_pair
        self.offset = -1 - 2 * first_pair
        self.d0 = -((self.pad + self.offset + 1) // 2)
        self.D = (self.pad - self.offset + 1) // 2 - self.d0 + 1
        assert self.d0 % 2 == 0 and self.D % 2 == 0
        self.ms = range(self.d0 // 2, self.d0 // 2 + self.D // 2)
        self.L = self.D + self.D // 2
        self.half = 2 * self.L
        self.row = 2 * self.half
        self.block = H * self.row
        self.windows = []
        for q in range(BANDS):
            first, last = HB * q, min(H, HB * q + HB) - 1
            self.windows.append((max(0, first - self.pad), min(H - 1, last + self.pad) + 1))
        self.margin = HB - 1
        self.rows = K + 2 * self.margin
        self.padded = self.rows * self.row
        self.pitch = (self.rows - self.margin) * self.row

    def taps(self, parity_in, parity_out):
        rest = parity_in - parity_out + self.offset + self.pad
        column = rest % 2
        return column, (column - rest) // 2 - self.d0, len(range(column, self.K, 2))

    def products(self):
        even, odd = (0, JE), (JE, JH)
        x0, x1 = (even, odd) if self.first_pair == 0 else (odd, even)
        return [
            (x0[0], 0, x0[1], JH + 1, [(m, 2 * m - self.d0) for m in self.ms]),
            (x1[0], self.first_pair, x1[1], JH, [(m, 2 * m + 1 - self.d0) for m in self.ms]),
            (2 * JE, -1, JE, JH, [(m, self.D + m - self.ms[0]) for m in self.ms]),
        ]


def slots(i):
    if isinstance(i, int) and i == 0:
        return FIRST_SLOTS
    if isinstance(i, int) and i == GROUPS:
        return SECOND_SLOTS
    return list(range(SLOTS))


def job(i, s):
    if isinstance(i, int) and i == 0:
        return FIRST_SLOTS.index(s)
    if isinstance(i, int) and i == GROUPS:
        return SLOTS * i - CG + SECOND_SLOTS.index(s)
    return i * SLOTS + (s - CG)


def channel(i, s):
    conv, c = PATTERN[s]
    return conv, (i if conv == FIRST else i - 1), c


def ring(i, s, size):
    return job(i if isinstance(i, int) else 1, s) % size


def later(i, s, k):
    here = slots(i)
    at = here.index(s) + k
    if at < len(here):
        return i, here[at]
    if isinstance(i, int) and i == GROUPS:
        return None
    return i + 1, slots(i + 1)[at - len(here)]


def earlier(i, s):
    here = slots(i)
    if s != here[0]:
        return i, here[here.index(s) - 1]
    if isinstance(i, int) and i == 0:
        return None
    return i - 1, slots(i - 1)[-1]


MEASURED = {0: [0], 1: [1], 3: [2, 3], 5: [4, 5]}
NORM1_SLOT = FIRST_SLOTS[-1]


def norm2_slot(i):
    if isinstance(i, int) and i in (0, GROUPS):
        return None
    if isinstance(i, int) and i == GROUPS - 1:
        return SLOTS - AHEAD
    return SLOTS - 1


def norm2_ordinal(i):
    return 2 * GROUPS - 1 if isinstance(i, int) and i == GROUPS - 1 else i * 2 + 2


def positive(value):
    return not isinstance(value, int) or value > 0


def conv_norm_kernel(nc, x, weight1, bias, coord, radius, weight2, out):
    f1, f2 = Filter(K1, -1), Filter(K2, 0)

    with ExitStack() as ctx:
        def sb(name, shape, dt=F32):
            return ctx.enter_context(nc.sbuf_tensor(name, shape, dt))

        def sem(name):
            return ctx.enter_context(nc.semaphore(name))

        raw = sb("raw", [P, X_RING, CG * RUN])
        scratch = sb("scratch", [P, HB * WP])
        xt = sb("xt", [P, B + N_X])
        xs = sb("xs", [P, JE * B])
        x_hi = sb("x_hi", [P, H_RING, N_OP], F32R)
        x_lo = sb("x_lo", [P, H_RING, N_OP], F32R)
        p0 = sb("p0", [P, (JH + 1) * B])
        p1 = sb("p1", [P, JH * B])
        yt = sb("yt", [P, N])
        toep1 = sb("toep1", [P, T_RING, f1.block], F32R)
        toep2 = sb("toep2", [P, T_RING, f2.block], F32R)
        bias_all = sb("bias_all", [P, C])
        part1 = sb("part1", [P, 2, CG, 6])
        part2 = sb("part2", [P, 2, CG, 6])
        norm1 = sb("norm1", [P, 2])
        norm2 = sb("norm2", [P, 2])
        agg = sb("agg", [P, 2, 2])
        halves = sb("halves", [B, 2, HALVES])
        halves_tmp = sb("halves_tmp", [B, 2, HALVES])
        small = sb("small", [B, 8])
        wait_carrier = sb("wait_carrier", [1, 1])

        w2_src = sb("w2_src", [CP, CT, POINTS])
        coord_all = sb("coord_all", [CP, POINTS * 2])
        radius_all = sb("radius_all", [CP, POINTS])
        lin = sb("lin", [CP, 2, K2])
        dist = sb("dist", [CP, 2, K2])
        dist_raw = sb("dist_raw", [CP, 2, K2])
        hat = sb("hat", [CP, K2 * K2])
        taps2 = sb("taps2", [CP, CT, K2 * K2])

        acc = ctx.enter_context(nc.psum_tensor("acc", [P, P_RING, 3, BANK], F32))

        padded1 = nc.dram_tensor("padded1", [C, 2, f1.padded], F32)
        padded2 = nc.dram_tensor("padded2", [C, 2, f2.padded], F32)

        x_landed = sem("x_landed")
        w_landed = sem("w_landed")
        params_landed = sem("params_landed")
        toep1_landed = [sem(f"toep1_landed{k}") for k in range(T_RING)]
        toep2_landed = [sem(f"toep2_landed{k}") for k in range(T_RING)]
        bufs_zeroed = sem("bufs_zeroed")
        area_zeroed = sem("area_zeroed")
        acc_zeroed = sem("acc_zeroed")
        last_band_zeroed = sem("last_band_zeroed")
        toep_zeroed = sem("toep_zeroed")
        taps_chain = sem("taps_chain")
        taps_laid = sem("taps_laid")
        w_hi_ready = sem("w_hi_ready")
        w_lo_ready = sem("w_lo_ready")
        padded_stored = sem("padded_stored")
        parts1_ready = sem("parts1_ready")
        parts2_ready = sem("parts2_ready")
        norm_chain = sem("norm_chain")
        var_ready = sem("var_ready")
        std_ready = sem("std_ready")
        xn_ready = sem("xn_ready")
        xt_ready = sem("xt_ready")
        xs_ready = sem("xs_ready")
        hi_ready = sem("hi_ready")
        lo_ready = sem("lo_ready")
        lo_sums_ready = sem("lo_sums_ready")
        conv_done = sem("conv_done")
        p01_done = sem("p01_done")
        p01_copied = sem("p01_copied")
        even_ready = sem("even_ready")
        odd_rest_ready = sem("odd_rest_ready")
        odd_ready = sem("odd_ready")
        y_ready = sem("y_ready")
        residual_added = sem("residual_added")
        out_stored = sem("out_stored")

        x_dram = x.rearrange("b (g c) h w -> b g c (h w)", c=CG)
        out_dram = out.rearrange("b (g c) h w -> b g c (h w)", c=CG)

        spare = raw[0:CP, 1:X_RING, :].rearrange("p g n -> p (g n)")
        area_size = f1.pitch + f1.padded
        area = spare[:, 0:area_size]
        w1_src = spare[:, area_size:area_size + CT * K1 * K1].rearrange("p (t n) -> p t n", t=CT)
        work_start = area_size + CT * K1 * K1
        work_size = K1 * 2 * f1.D

        def work(f, e):
            start = work_start + e * work_size
            return spare[:, start:start + f.K * 2 * f.D].rearrange("p (k o d) -> p k o d", o=2, d=f.D)

        def work_sums(f):
            start = work_start + 2 * work_size
            return spare[:, start:start + f.K * f.D].rearrange("p (k o d) -> p k o d", o=2, d=f.D // 2)

        def padded(f, place):
            start = 0 if f is f1 else area_size - (3 * f2.pitch + f2.padded)
            return area[:, start + place * f.pitch:start + place * f.pitch + f.padded]

        def padded_rows(f, place, part):
            rows = padded(f, place).rearrange("p (r o e m) -> p r o e m", o=2, e=2, m=f.L)
            return rows[:, f.margin:f.margin + f.K, :, part, :]

        STAGES = [[(f1, 0, 0)], [(f1, 1, 0)], [(f2, 0, 0), (f2, 1, 2)]]
        LAID = [2 * sum(len(x) for x in STAGES[:k + 1]) for k in range(len(STAGES))]

        STORED = [2 + x for x in LAID]

        def x0_x1(tile):
            return tile.rearrange("p (j s b) -> p s j b", s=2, b=B)

        def apart(tile):
            return tile[:, 0:N_X].rearrange("p (s j b) -> p s j b", s=2, b=B)

        padded_image = scratch[:].rearrange("p (h w) -> p h w", w=WP)
        image = padded_image[:, :, 1:1 + W]

        def raw_rows(g, c):
            return raw_channel(g, c).rearrange("p (h w) -> p h w", w=W)

        def raw_channel(g, c):
            return raw[:, g % X_RING, c * RUN:(c + 1) * RUN]

        def band_rows(q):
            return HB if q < BANDS - 1 else HB_LAST

        def raw_band(g, q, c0, c1):
            return raw[B * q:B * q + B, g % X_RING, c0 * RUN:c1 * RUN].rearrange(
                "p (c n) -> p c n", n=RUN)[:, :, 0:band_rows(q) * W]

        def dram_band(images, g, q, c0, c1):
            return images[:, g, c0:c1, q * RUN:q * RUN + band_rows(q) * W]

        def blocks(tile):
            return tile.rearrange("p h (j e) -> p j h e", e=2)

        block = ctx.enter_context(nc.Block())

        @block.sync
        def _(sp):
            def load_x(g):
                for q in range(BANDS):
                    sp.dma_start(raw_band(g, q, 0, CG), dram_band(x_dram, g, q, 0, CG)).then_inc(x_landed, 16)

            def load_toeplitz(m, place, f, padded, toep, landed):
                for q in range(BANDS):
                    (lo, hi), rows = f.windows[q], band_rows(q)
                    first = HB - rows
                    src = bass.AP(padded, m * (2 * f.padded) + (lo - HB * q + f.pad + first) * f.row,
                                  [[f.row, rows], [f.padded, 2], [1, (hi - lo) * f.row]])
                    sp.dma_start(toep[2 * (HB * q + first):2 * HB * (q + 1), place, lo * f.row:hi * f.row].bitcast(F32), src
                                 ).then_inc(landed[place], 16)

            def load_toeplitz1(m, place):
                load_toeplitz(m, place, f1, padded1, toep1, toep1_landed)

            def load_toeplitz2(m, place):
                load_toeplitz(m, place, f2, padded2, toep2, toep2_landed)

            def store(g, c0, c1):
                for q in range(BANDS):
                    sp.dma_start(dram_band(out_dram, g, q, c0, c1), raw_band(g, q, c0, c1)).then_inc(out_stored, 16)

            sp.dma_start(w1_src, weight1.rearrange("(t p) o h w -> p t (o h w)", p=CP)).then_inc(w_landed, 16)
            load_x(0)
            sp.dma_start(w2_src[:], weight2.rearrange("o (t p) n -> p t (o n)", p=CP)).then_inc(params_landed, 16)
            sp.dma_start(coord_all[:], coord.rearrange("o n e -> o (n e)").to_broadcast([CP, POINTS * 2])).then_inc(params_landed, 16)
            sp.dma_start(radius_all[:], radius.rearrange("o n a b -> o (n a b)").to_broadcast([CP, POINTS])).then_inc(params_landed, 16)
            sp.dma_start(bias_all[:], bias.rearrange("(o c) -> o c", o=1).to_broadcast([P, C])).then_inc(params_landed, 16)

            def store_filters(k, first=0, last=CP):
                sp.wait_ge(w_lo_ready, 2 * LAID[k])
                for f, t, place in STAGES[k]:
                    target = padded1 if f is f1 else padded2
                    for e in range(2):
                        sp.dma_start(target[t * CP + first:t * CP + last, e, :], padded(f, place + e)[first:last, :]
                                     ).then_inc(padded_stored, 16)

            store_filters(0, 0, CG)
            sp.wait_ge(padded_stored, 16 * 2)
            sp.wait_ge(toep_zeroed, 2)
            for m in range(T_RING):
                load_toeplitz1(m, m)
            store_filters(0, CG, CP)

            def filters_and_first_loads(k):
                if k == 2:
                    store_filters(1)
                if k == 3:
                    sp.wait_ge(padded_stored, 16 * STORED[1])
                    sp.wait_ge(x_landed, 16 * BANDS)
                    load_x(1)
                if k == 4:
                    store_filters(2)
                if k == 5:
                    sp.wait_ge(padded_stored, 16 * STORED[2])
                    for m in range(T_RING):
                        load_toeplitz2(m, m)
                    sp.wait_ge(x_landed, 16 * BANDS * 2)
                    load_x(2)

            def next_toeplitz(i, s):
                conv, g, c = channel(i, s)
                m = g * CG + (c + T_RING)
                if not isinstance(m, int) or m < C:
                    (load_toeplitz1 if conv == FIRST else load_toeplitz2)(m, c % T_RING)

            def iteration(i):
                first = isinstance(i, int) and i == 0
                for s in slots(i):
                    n = job(i, s)
                    if positive(n):
                        sp.wait_ge(conv_done, n)
                        next_toeplitz(*earlier(i, s))
                    if first:
                        filters_and_first_loads(n)
                    if s == 1 and not (isinstance(i, int) and i < 2):
                        sp.wait_ge(residual_added, job(i, 0))
                        store(i - 2, CG // 2, CG)
                    if s == 4 and not (isinstance(i, int) and i + 2 >= GROUPS):
                        if positive(i - 1):
                            sp.wait_ge(out_stored, (i - 1) * (16 * BANDS * 2))
                        sp.wait_ge(x_landed, (i + 2) * (16 * BANDS))
                        load_x(i + 2)
                    if s == SECOND_SLOTS[CG // 2 - 1] + 2 and not first:
                        sp.wait_ge(residual_added, job(i, s - 2) + 1)
                        store(i - 1, 0, CG // 2)

            iteration(0)
            iteration(1)
            with sp.Fori(2, GROUPS - 2) as i:
                iteration(i)
            iteration(GROUPS - 2)
            iteration(GROUPS - 1)
            sp.wait_ge(residual_added, SLOTS * GROUPS - CG)
            store(GROUPS - 2, CG // 2, CG)
            iteration(GROUPS)
            sp.wait_ge(residual_added, SLOTS * GROUPS)
            store(GROUPS - 1, CG // 2, CG)
            sp.wait_ge(out_stored, 16 * BANDS * 2 * GROUPS)

        @block.gpsimd
        def _(pool):
            def zero_last_band(g0, g1):
                missing = raw[B * (BANDS - 1):P, g0:g1].rearrange("p g (c n) -> p (g c) n", n=RUN)[:, :, HALF:RUN]
                nc.gpsimd.memset(missing, 0.0).then_inc(last_band_zeroed, 1)

            nc.gpsimd.memset(area[:, area_size // 2:], 0.0).then_inc(area_zeroed, 1)
            pool.wait_ge(area_zeroed, 1)
            nc.gpsimd.memset(toep1[:].bitcast(F32), 0.0).then_inc(toep_zeroed, 1)
            nc.gpsimd.memset(toep2[:].bitcast(F32), 0.0).then_inc(toep_zeroed, 1)
            pool.wait_ge(toep_zeroed, 2)
            zero_last_band(0, 1)
            pool.wait_ge(last_band_zeroed, 1)
            zero_last_band(1, X_RING)
            pool.wait_ge(last_band_zeroed, 2)

            def combine(i, s):
                n = job(i, s)
                pool.wait_ge(p01_copied, n * 2 + 2)
                if positive(n):
                    pool.wait_ge(y_ready, n)
                nc.gpsimd.tensor_tensor(x0_x1(yt[:])[:, 0], p0[:, 0:JH * B].rearrange("p (j b) -> p j b", b=B),
                                        p1[:].rearrange("p (j b) -> p j b", b=B), ALU.add).then_inc(even_ready, 1)
                pool.wait_ge(even_ready, n + 1)
                nc.gpsimd.tensor_tensor(p1[:], p0[:, B:(JH + 1) * B], p1[:], ALU.add).then_inc(odd_rest_ready, 1)

            def add_pairs(i, s):
                n = job(i, s)
                pool.wait_ge(xt_ready, n + 1)
                if positive(n):
                    pool.wait_ge(lo_sums_ready, n)
                start = B if PATTERN[s][0] == FIRST else 0
                pairs = x0_x1(xt[:, start:start + N_X])
                nc.gpsimd.tensor_tensor(xs[:].rearrange("p (j b) -> p j b", b=B), pairs[:, 0], pairs[:, 1], ALU.add
                                        ).then_inc(xs_ready, 1)

            def low_sums(i, s):
                n = job(i, s)
                h = ring(i, s, H_RING)
                pool.wait_ge(hi_ready, n * 2 + 2)
                nc.gpsimd.tensor_tensor(x_lo[:, h, N_X:N_OP], xs[:], x_hi[:, h, N_X:N_OP].bitcast(F32), ALU.subtract
                                        ).then_inc(lo_sums_ready, 1)

            for s in slots(0)[:AHEAD]:
                add_pairs(0, s)
                low_sums(0, s)

            def iteration(i):
                for s in slots(i):
                    combine(i, s)
                    after = later(i, s, AHEAD)
                    if after:
                        add_pairs(*after)
                        low_sums(*after)

            iteration(0)
            with pool.Fori(1, GROUPS - 1) as i:
                iteration(i)
            iteration(GROUPS - 1)
            iteration(GROUPS)

        @block.scalar
        def _(act):
            def high_part(i, s):
                n = job(i, s)
                act.wait_ge(xt_ready, n + 1)
                if positive(n - (H_RING - 1)):
                    act.wait_ge(conv_done, n - (H_RING - 1))
                h = ring(i, s, H_RING)
                nc.scalar.activation(apart(x_hi[:, h, :]), x0_x1(xt[:, B:B + N_X]), ACT.Copy).then_inc(hi_ready, 1)
                act.wait_ge(xs_ready, n + 1)
                nc.scalar.activation(x_hi[:, h, N_X:N_OP], xs[:], ACT.Copy).then_inc(hi_ready, 1)

            def copy_products(i, s):
                n = job(i, s)
                act.wait_ge(p01_done, n + 1)
                if positive(n):
                    act.wait_ge(odd_ready, n)
                acc_n = acc[:, ring(i, s, P_RING)]
                nc.scalar.activation(p0[:], acc_n[:, 0, 0:(JH + 1) * B], ACT.Copy).then_inc(p01_copied, 1)
                nc.scalar.activation(p1[:], acc_n[:, 1, 0:JH * B], ACT.Copy).then_inc(p01_copied, 1)

            def root(f):
                act.wait_ge(var_ready, f + 1)
                nc.scalar.activation(small[:, 5:6], small[:, 4:5], ACT.Sqrt).then_inc(std_ready, 1)

            def filters_high(k):
                done = LAID[k] - 2 * len(STAGES[k])
                if k > 0:
                    act.wait_ge(padded_stored, 16 * STORED[k - 1])
                else:
                    act.wait_ge(area_zeroed, 1)
                for f, t, place in STAGES[k]:
                    for e in range(2):
                        done += 1
                        act.wait_ge(taps_laid, done)
                        dst = padded_rows(f, place + e, 0).bitcast(F32R)
                        nc.scalar.activation(dst[:, :, :, 0:f.D], work(f, e), ACT.Copy).then_inc(w_hi_ready, 1)
                        nc.scalar.activation(dst[:, :, :, f.D:f.L], work_sums(f), ACT.Copy).then_inc(w_hi_ready, 1)

            filters_high(0)
            root(0)
            for s in slots(0)[:AHEAD]:
                high_part(0, s)

            def iteration(i):
                peeled = isinstance(i, int)
                for s in slots(i):
                    copy_products(i, s)
                    if s == NORM1_SLOT and not (peeled and (i == 0 or i >= GROUPS - 1)):
                        root(i * 2 + 1)
                    if s == norm2_slot(i):
                        root(norm2_ordinal(i))
                    after = later(i, s, AHEAD)
                    if after:
                        high_part(*after)
                    if peeled and i == 0:
                        k = job(i, s)
                        if k == CG - 1 - AHEAD:
                            root(1)
                        if k in (0, 2):
                            filters_high(k // 2 + 1)
                        if k == CG - 1:
                            root(2)

            iteration(0)
            with act.Fori(1, GROUPS - 1) as i:
                iteration(i)
            iteration(GROUPS - 1)
            iteration(GROUPS)

        @block.vector
        def _(dve):
            def normalisation(f, g, parts, parts_ready, norm):
                done = [0]

                def link(ins):
                    done[0] += 1
                    ins.then_inc(norm_chain, 1)

                def settle():
                    dve.wait_ge(norm_chain, f * NORM_STEPS + done[0])

                dve.wait_ge(parts_ready, (g + 1) * (2 * CG))
                nc.vector.memset(small[:, 1:2], 0.0)
                link(nc.vector.bn_aggr(agg[:, 0, :], parts[:, 0].rearrange("p c k -> p (c k)")))
                link(nc.vector.bn_aggr(agg[0:B * (BANDS - 1), 1, :],
                                       parts[0:B * (BANDS - 1), 1].rearrange("p c k -> p (c k)")))
                settle()
                for k in range(HALVES):
                    q = k // 2
                    link(nc.vector.tensor_copy(halves[:, :, k], agg[B * q:B * q + B, k % 2, :]))
                settle()
                link(nc.vector.tensor_reduce(small[:, 0:1], halves[:, 0, :], AX_X, ALU.add))
                settle()
                link(nc.vector.tensor_scalar(small[:, 6:7], small[:, 0:1], 1.0 / HALVES, None, ALU.mult))
                settle()
                link(nc.vector.tensor_scalar(halves_tmp[:, 0, :], halves[:, 0, :], small[:, 6:7], None, ALU.subtract))
                settle()
                link(nc.vector.tensor_tensor(halves_tmp[:, 1, :], halves_tmp[:, 0, :], halves_tmp[:, 0, :], ALU.mult))
                settle()
                link(nc.vector.tensor_tensor(halves_tmp[:, 0, :], halves_tmp[:, 1, :], halves[:, 1, :], ALU.add))
                settle()
                link(nc.vector.tensor_reduce(small[:, 3:4], halves_tmp[:, 0, :], AX_X, ALU.add))
                settle()
                nc.vector.tensor_scalar(small[:, 4:5], small[:, 3:4], 1.0 / HALVES, EPS, ALU.mult, ALU.add).then_inc(var_ready, 1)
                dve.wait_ge(std_ready, f + 1)
                link(nc.vector.reciprocal(small[:, 7:8], small[:, 5:6]))
                settle()
                link(nc.vector.tensor_tensor(small[:, 0:1], small[:, 7:8], small[:, 7:8], ALU.mult))
                settle()
                link(nc.vector.tensor_tensor(small[:, 3:4], small[:, 0:1], small[:, 4:5], ALU.mult))
                settle()
                link(nc.vector.tensor_scalar(small[:, 0:1], small[:, 3:4], -0.5, 1.5, ALU.mult, ALU.add))
                settle()
                link(nc.vector.tensor_tensor(small[:, 7:8], small[:, 7:8], small[:, 0:1], ALU.mult))
                settle()
                for q in range(BANDS):
                    link(nc.vector.tensor_copy(norm[B * q:B * q + B, :], small[:, 6:8]))
                settle()
                assert done[0] == NORM_STEPS

            def statistics(parts, parts_ready, g, c):
                for k in range(2):
                    held = P if k == 0 else B * (BANDS - 1)
                    nc.vector.bn_stats(parts[0:held, k, c, :], raw_channel(g, c)[0:held, k * HALF:(k + 1) * HALF]
                                       ).then_inc(parts_ready, 1)

            def prepare(i, s):
                n = job(i, s)
                conv, g, c = channel(i, s)
                norm = norm1 if conv == FIRST else norm2
                if positive(n):
                    dve.wait_ge(xt_ready, n)
                if positive(n - AHEAD):
                    dve.wait_ge(residual_added, n - AHEAD)
                nc.vector.tensor_scalar(image, raw_rows(g, c), norm[:, 0:1], norm[:, 1:2],
                                        ALU.subtract, ALU.mult).then_inc(xn_ready, 1)
                dve.wait_ge(xn_ready, n + 1)
                if positive(n):
                    dve.wait_ge(lo_ready, n)
                    dve.wait_ge(xs_ready, n)
                nc.vector.transpose(xt[:, B:B + (JW + 1) * B].rearrange("p (j b) -> p j b", b=B),
                                    blocks(padded_image)[:, :, ::-1, :]).then_inc(xt_ready, 1)

            def low_part(i, s):
                n = job(i, s)
                h = ring(i, s, H_RING)
                dve.wait_ge(hi_ready, n * 2 + 1)
                nc.vector.tensor_tensor(apart(x_lo[:, h, :]), x0_x1(xt[:, B:B + N_X]),
                                        apart(x_hi[:, h, :].bitcast(F32)), ALU.subtract).then_inc(lo_ready, 1)

            def bring_back(i, s, prepared):
                n = job(i, s)
                dve.wait_ge(conv_done, n + 1)
                dve.wait_ge(odd_rest_ready, n + 1)
                nc.vector.tensor_tensor(x0_x1(yt[:])[:, 1],
                                        acc[:, ring(i, s, P_RING), 2, 0:JH * B].rearrange("p (j b) -> p j b", b=B),
                                        p1[:].rearrange("p (j b) -> p j b", b=B), ALU.subtract).then_inc(odd_ready, 1)
                dve.wait_ge(odd_ready, n + 1)
                dve.wait_ge(xt_ready, prepared)
                if positive(n):
                    dve.wait_ge(residual_added, n)
                nc.vector.transpose(blocks(image), yt[:].rearrange("p (j b) -> p j b", b=B)).then_inc(y_ready, 1)

            def add_residual(i, s):
                n = job(i, s)
                conv, g, c = channel(i, s)
                dve.wait_ge(y_ready, n + 1)
                if conv == FIRST:
                    nc.vector.scalar_tensor_tensor(raw_rows(g, c), image, bias_all[:, bass.ds(g * CG + c, 1)],
                                                   raw_rows(g, c), ALU.add, ALU.add).then_inc(residual_added, 1)
                else:
                    nc.vector.tensor_tensor(raw_rows(g, c), image, raw_rows(g, c), ALU.add
                                            ).then_inc(residual_added, 1)

            nc.vector.memset(area[:, 0:area_size // 2], 0.0).then_inc(bufs_zeroed, 1)
            nc.vector.memset(spare[:, work_start:work_start + 2 * work_size], 0.0).then_inc(bufs_zeroed, 1)
            nc.vector.memset(xt[:, 0:B], 0.0).then_inc(bufs_zeroed, 1)
            nc.vector.memset(xt[:, N_X:], 0.0).then_inc(bufs_zeroed, 1)
            nc.vector.memset(padded_image[:, :, ::WP - 1], 0.0).then_inc(bufs_zeroed, 1)
            dve.wait_ge(bufs_zeroed, 5)

            steps = [0]

            def step(ins):
                steps[0] += 1
                ins.then_inc(taps_chain, 1)
                dve.wait_ge(taps_chain, steps[0])

            def taps_11x11():
                for k in range(K2):
                    at = -1.0 + 2.0 * k / (K2 - 1)
                    nc.vector.memset(lin[:, 0, k:k + 1], at)
                    step(nc.vector.memset(lin[:, 1, K2 - 1 - k:K2 - k], at))
                dve.wait_ge(params_landed, 16 * 4)
                step(nc.vector.reciprocal(radius_all[:], radius_all[:]))
                for p in range(POINTS):
                    for axis in range(2):
                        step(nc.vector.tensor_scalar(dist_raw[:, axis, :], lin[:, axis, :],
                                                     coord_all[:, 2 * p + axis:2 * p + axis + 1], None, ALU.subtract))
                    step(nc.vector.scalar_tensor_tensor(dist[:], dist_raw[:], -1.0, dist_raw[:], ALU.mult, ALU.max))
                    grid = hat[:].rearrange("p (h w) -> p h w", w=K2)
                    step(nc.vector.tensor_tensor(grid, dist[:, 0, :].unsqueeze(1).to_broadcast([CP, K2, K2]),
                                                 dist[:, 1, :].unsqueeze(2).to_broadcast([CP, K2, K2]), ALU.add))
                    step(nc.vector.tensor_scalar(hat[:], hat[:], radius_all[:, p:p + 1], -1.0, ALU.mult, ALU.mult))
                    step(nc.vector.tensor_scalar(hat[:], hat[:], 1.0, 0.0, ALU.add, ALU.max))
                    for t in range(CT):
                        if p == 0:
                            step(nc.vector.tensor_scalar(taps2[:, t, :], hat[:], w2_src[:, t, p:p + 1], None, ALU.mult))
                        else:
                            step(nc.vector.scalar_tensor_tensor(taps2[:, t, :], hat[:], w2_src[:, t, p:p + 1], taps2[:, t, :],
                                                                ALU.mult, ALU.add))

            def filters_low(k):
                done = LAID[k] - 2 * len(STAGES[k])
                if k > 0:
                    dve.wait_ge(padded_stored, 16 * STORED[k - 1])
                if k == 2:
                    step(nc.vector.memset(area[:, area_size - (3 * f2.pitch + f2.padded):], 0.0))
                    step(nc.vector.memset(spare[:, work_start:work_start + 2 * work_size], 0.0))
                for f, t, place in STAGES[k]:
                    taps = (w1_src if f is f1 else taps2)[:, t, :].rearrange("p (h w) -> p h w", w=f.K)
                    for e in range(2):
                        done += 1
                        for o in range(2):
                            column, first, count = f.taps(e, o)
                            step(nc.vector.tensor_copy(work(f, e)[:, :, o, first:first + count],
                                                       taps[:, ::-1, column:column + 2 * count - 1:2]))
                        pairs = work(f, e).rearrange("p k o (m s) -> p k o s m", s=2)
                        for o in range(2):
                            step(nc.vector.tensor_tensor(work_sums(f)[:, :, o, :], pairs[:, :, o, 0, :],
                                                         pairs[:, :, o, 1, :], ALU.add))
                        nc.vector.memset(small[:, 2:3], 0.0).then_inc(taps_laid, 1)
                        dve.wait_ge(w_hi_ready, 2 * done)
                        low, high = padded_rows(f, place + e, 1).bitcast(F32R), padded_rows(f, place + e, 0)
                        nc.vector.tensor_tensor(low[:, :, :, 0:f.D], work(f, e),
                                                high[:, :, :, 0:f.D], ALU.subtract).then_inc(w_lo_ready, 1)
                        nc.vector.tensor_tensor(low[:, :, :, f.D:f.L], work_sums(f), high[:, :, :, f.D:f.L], ALU.subtract
                                                ).then_inc(w_lo_ready, 1)
                        dve.wait_ge(w_lo_ready, 2 * done)

            dve.wait_ge(w_landed, 16)
            filters_low(0)

            nc.vector.memset(acc[B * (BANDS - 1):P], 0.0).then_inc(acc_zeroed, 1)

            dve.wait_ge(x_landed, 16 * BANDS)
            for c in range(CG):
                statistics(part1, parts1_ready, 0, c)
            normalisation(0, 0, part1, parts1_ready, norm1)
            dve.wait_ge(last_band_zeroed, 1)
            for s in slots(0)[:AHEAD]:
                prepare(0, s)
                low_part(0, s)

            taps_11x11()

            def iteration(i):
                peeled = isinstance(i, int)
                for s in slots(i):
                    conv, g, c = channel(i, s)
                    after = later(i, s, AHEAD)
                    measure_next = not (peeled and (i == 0 or i >= GROUPS - 1))
                    if s == 0 and measure_next:
                        dve.wait_ge(x_landed, (i + 2) * (16 * BANDS))
                    if s == norm2_slot(i):
                        normalisation(norm2_ordinal(i), i, part2, parts2_ready, norm2)
                    if after:
                        prepare(*after)
                    if measure_next:
                        for c1 in MEASURED.get(s, []):
                            statistics(part1, parts1_ready, i + 1, c1)
                        if s == NORM1_SLOT:
                            normalisation(i * 2 + 1, i + 1, part1, parts1_ready, norm1)
                    n = job(i, s)
                    bring_back(i, s, min(n + 1 + AHEAD, SLOTS * GROUPS) if isinstance(n, int) else n + (1 + AHEAD))
                    if after:
                        low_part(*after)
                    add_residual(i, s)
                    if conv == FIRST:
                        dve.wait_ge(residual_added, job(i, s) + 1)
                        nc.vector.memset(wait_carrier[:], 0.0)
                        statistics(part2, parts2_ready, i, c)
                    if peeled and n == CG - 1 - AHEAD:
                        dve.wait_ge(last_band_zeroed, 2)
                        dve.wait_ge(x_landed, 16 * BANDS * 2)
                        for c1 in range(CG):
                            statistics(part1, parts1_ready, 1, c1)
                        normalisation(1, 1, part1, parts1_ready, norm1)
                    if peeled and n in (0, 2):
                        filters_low(n // 2 + 1)
                if peeled and i == 0:
                    normalisation(2, 0, part2, parts2_ready, norm2)

            iteration(0)
            with dve.Fori(1, GROUPS - 1) as i:
                iteration(i)
            iteration(GROUPS - 1)
            iteration(GROUPS)

        @block.tensor
        def _(pe):
            pe.wait_ge(acc_zeroed, 1)

            def toeplitz(toep, f, place, part, k):
                return bass.AP(toep, place * f.block + part * f.L + k, [[T_RING * f.block, P], [f.half, M]])

            def convolve(i, s, f, toep, place):
                h, p = ring(i, s, H_RING), ring(i, s, P_RING)
                for bank, (start, j_in, n_in, n_out, matrices) in enumerate(f.products()):
                    if bank == 2:
                        pe.wait_ge(lo_sums_ready, job(i, s) + 1)
                    matrices = sorted(matrices, key=lambda x: abs(x[0]))
                    for m, k in matrices:
                        j0, j1 = max(0, j_in - m), min(n_out, j_in + n_in - m)
                        dst = acc[0:M, p, bank, j0 * B:j1 * B]
                        cols = slice((start + j0 + m - j_in) * B, (start + j1 + m - j_in) * B)
                        for part, src in ((0, x_hi), (0, x_lo), (1, x_hi)):
                            last = nc.tensor.matmul(dst, toeplitz(toep, f, place, part, k), src[:, h, cols],
                                                    start=(m == 0 and part == 0 and src is x_hi),
                                                    stop=(m == matrices[-1][0] and part == 1), skip_group_check=True)
                    if bank == 1:
                        last.then_inc(p01_done, 1)
                return last

            def iteration(i):
                for s in slots(i):
                    n = job(i, s)
                    pe.wait_ge(lo_ready, n + 1)
                    if positive(n + 1 - P_RING):
                        pe.wait_ge(odd_ready, n + 1 - P_RING)
                    conv, g, c = channel(i, s)
                    f, toep, landed = (f1, toep1, toep1_landed) if conv == FIRST else (f2, toep2, toep2_landed)
                    pe.wait_ge(landed[c % T_RING], g * (16 * BANDS * CG // T_RING) + 16 * BANDS * (c // T_RING + 1))
                    last = convolve(i, s, f, toep, c % T_RING)
                    last.then_inc(conv_done, 1)

            iteration(0)
            with pe.Fori(1, GROUPS - 1) as i:
                iteration(i)
            iteration(GROUPS - 1)
            iteration(GROUPS)


_INS = ["x", "L0_conv_weight", "L0_conv_bias_term", "L1_conv_weight_coord", "L1_conv_radius", "L1_conv_weights"]


def kernel(**inputs):
    import numpy as _np
    import concourse.bacc as _bacc
    from concourse.bass_utils import run_bass_kernel_spmd as _run

    nc = _bacc.Bacc("TRN2", target_bir_lowering=False, num_devices=1)
    arrays, args = {}, []
    for name in _INS:
        a = _np.ascontiguousarray(inputs[name])
        arrays[f"in_{name}_dram"] = a
        args.append(nc.dram_tensor(f"in_{name}_dram", a.shape, mybir.dt.from_np(a.dtype), kind="ExternalInput").ap())
    out = nc.dram_tensor("out_0_dram", (B, C, H, W), F32, kind="ExternalOutput").ap()
    conv_norm_kernel(nc, *args, out)
    r = _run(nc, [arrays], core_ids=[0])
    return r.results[0]["out_0_dram"]
```
